# Optimizing a Trainium2 kernel written in Bass

```python
import numpy as np
import jax
import jax.numpy as jnp

def _softmax(x, axis=-1):
    return jax.nn.softmax(x, axis=axis)

def _gelu(x):
    return jax.nn.gelu(x, approximate=True)

def _silu(x):
    return jax.nn.silu(x)

def _sigmoid(x):
    return jax.nn.sigmoid(x)

def _layernorm(x, axis=-1, eps=1e-05):
    m = jnp.mean(x, axis=axis, keepdims=True)
    v = jnp.var(x, axis=axis, keepdims=True)
    return (x - m) / jnp.sqrt(v + eps)

def _scatter_add(tgt, idx, src, axis=0):
    return tgt.at[idx].add(src)

def _segment_sum(src, seg, n):
    return jax.ops.segment_sum(src, seg, n)
kernel_name = 'mk_xattn_seq_d1_seqx_r4_59430a'

def setup_inputs(seed: int=0):
    np.random.seed(seed)
    _w = jnp.asarray

    def _rec_inputs():
        import jax
        import jax.numpy as jnp
        _rk = jax.random.key(seed)
        x = -0.0002928 + 1 * jax.random.normal(jax.random.fold_in(_rk, 1), (32, 128, 512), jnp.float32)
        _lenS = 128 - jax.random.randint(jax.random.fold_in(_rk, 7), (32,), 0, max(1, 128 // 4) + 1, jnp.int32)
        _lenS2 = 128 - jax.random.randint(jax.random.fold_in(_rk, 8), (32,), 0, max(1, 128 // 4) + 1, jnp.int32)
        _ctx_2048P = jax.random.normal(jax.random.fold_in(_rk, 11), (32, 16, 512), jnp.float32)
        _ctx_2048c = jax.random.dirichlet(jax.random.fold_in(_rk, 511), 0.3 * jnp.ones((16,), jnp.float32), (32, 128))
        _ctx_2048t = jnp.einsum('bsk,bkd->bsd', _ctx_2048c, _ctx_2048P)
        _ctx_2048t = _ctx_2048t * jax.lax.rsqrt(jnp.mean(jnp.square(_ctx_2048t)) + 1e-12) * 0.953939
        ctx_2048 = -1.39393e-06 + 0.999914 * (_ctx_2048t + 0.3 * jax.random.normal(jax.random.fold_in(_rk, 611), (32, 128, 512), jnp.float32))
        _validS = jnp.arange(128)[None, :] < _lenS[:, None]
        _validS2 = jnp.arange(128)[None, :] < _lenS2[:, None]
        _causal = jnp.tril(jnp.ones((128, 128), dtype=bool))
        mask_1x1xSxS2_fc1 = jnp.where(jnp.broadcast_to(_validS2[0:1, None, None, :], (1, 1, 128, 128)), 1.0, 0.0).astype(jnp.float32)
        mask_Bx1xSxS2_ff1 = jnp.where(jnp.ones((32, 1, 128, 128), dtype=bool), 1.0, 0.0).astype(jnp.float32)
        return (x, ctx_2048, mask_1x1xSxS2_fc1, mask_Bx1xSxS2_ff1)
    x, ctx_2048, mask_1x1xSxS2_fc1, mask_Bx1xSxS2_ff1 = _rec_inputs()

    def _L0_xattn_setup():
        import jax, jax.numpy as jnp
        import numpy as np
        H = 512
        NH = 16
        HD = H // NH
        EPS = 1e-05

        def gelu(x):
            return 0.5 * x * (1.0 + jnp.tanh(0.7978845608028654 * x * (1.0 + 0.044715 * x * x)))

        def layernorm(x, scale, bias):
            m = jnp.mean(x, axis=-1, keepdims=True)
            v = jnp.mean(jnp.square(x - m), axis=-1, keepdims=True)
            return (x - m) * jax.lax.rsqrt(v + EPS) * scale + bias

        def split_heads(x):
            b, s, _ = x.shape
            return x.reshape(b, s, NH, HD).transpose(0, 2, 1, 3)

        def merge_heads(x):
            b, nh, s, hd = x.shape
            return x.transpose(0, 2, 1, 3).reshape(b, s, nh * hd)

        def attention(q, k, v, mask):
            scores = jnp.einsum('bhqd,bhkd->bhqk', q, k) / jnp.sqrt(jnp.float32(HD))
            scores = scores * mask - 10000.0 * (1.0 - mask)
            probs = jax.nn.softmax(scores, axis=-1)
            return jnp.einsum('bhqk,bhkd->bhqd', probs, v)
        key = jax.random.key(seed)
        ks = jax.random.split(key, 16)
        b, s, t = (2, 256, 256)
        w = lambda k, i, o: jax.random.normal(k, (i, o), jnp.float32) * 0.02
        inp = {'hidden_states': jax.random.normal(ks[0], (b, s, H), jnp.float32), 'encoder_states': jax.random.normal(ks[1], (b, t, H), jnp.float32), 'ltor_mask': jnp.tril(jnp.ones((1, 1, s, s), jnp.float32)), 'cross_mask': jnp.ones((b, 1, s, t), jnp.float32), 'ln1_s': jnp.ones((H,), jnp.float32), 'ln1_b': jnp.zeros((H,), jnp.float32), 'w_qkv': w(ks[2], H, 3 * H), 'b_qkv': jnp.zeros((3 * H,), jnp.float32), 'w_ao': w(ks[3], H, H), 'b_ao': jnp.zeros((H,), jnp.float32), 'ln2_s': jnp.ones((H,), jnp.float32), 'ln2_b': jnp.zeros((H,), jnp.float32), 'w_q': w(ks[4], H, H), 'b_q': jnp.zeros((H,), jnp.float32), 'w_kv': w(ks[5], H, 2 * H), 'b_kv': jnp.zeros((2 * H,), jnp.float32), 'w_co': w(ks[6], H, H), 'b_co': jnp.zeros((H,), jnp.float32), 'ln3_s': jnp.ones((H,), jnp.float32), 'ln3_b': jnp.zeros((H,), jnp.float32), 'w1': w(ks[7], H, 4 * H), 'b1': jnp.zeros((4 * H,), jnp.float32), 'w2': w(ks[8], 4 * H, H), 'b2': jnp.zeros((H,), jnp.float32)}
        return inp
    _L0_xattn_all = _L0_xattn_setup()
    _L0_xattn_in = {k: v for k, v in _L0_xattn_all.items() if k in ('ln1_s', 'ln1_b', 'w_qkv', 'b_qkv', 'w_ao', 'b_ao', 'ln2_s', 'ln2_b', 'w_q', 'b_q', 'w_kv', 'b_kv', 'w_co', 'b_co', 'ln3_s', 'ln3_b', 'w1', 'b1', 'w2', 'b2')}
    del _L0_xattn_all
    return {'x': x, 'ctx_2048': ctx_2048, 'mask_1x1xSxS2_fc1': mask_1x1xSxS2_fc1, 'mask_Bx1xSxS2_ff1': mask_Bx1xSxS2_ff1, 'L0_xattn_ln1_s': _L0_xattn_in['ln1_s'], 'L0_xattn_ln1_b': _L0_xattn_in['ln1_b'], 'L0_xattn_w_qkv': _L0_xattn_in['w_qkv'], 'L0_xattn_b_qkv': _L0_xattn_in['b_qkv'], 'L0_xattn_w_ao': _L0_xattn_in['w_ao'], 'L0_xattn_b_ao': _L0_xattn_in['b_ao'], 'L0_xattn_ln2_s': _L0_xattn_in['ln2_s'], 'L0_xattn_ln2_b': _L0_xattn_in['ln2_b'], 'L0_xattn_w_q': _L0_xattn_in['w_q'], 'L0_xattn_b_q': _L0_xattn_in['b_q'], 'L0_xattn_w_kv': _L0_xattn_in['w_kv'], 'L0_xattn_b_kv': _L0_xattn_in['b_kv'], 'L0_xattn_w_co': _L0_xattn_in['w_co'], 'L0_xattn_b_co': _L0_xattn_in['b_co'], 'L0_xattn_ln3_s': _L0_xattn_in['ln3_s'], 'L0_xattn_ln3_b': _L0_xattn_in['ln3_b'], 'L0_xattn_w1': _L0_xattn_in['w1'], 'L0_xattn_b1': _L0_xattn_in['b1'], 'L0_xattn_w2': _L0_xattn_in['w2'], 'L0_xattn_b2': _L0_xattn_in['b2']}

def reference(x, ctx_2048, mask_1x1xSxS2_fc1, mask_Bx1xSxS2_ff1, L0_xattn_ln1_s, L0_xattn_ln1_b, L0_xattn_w_qkv, L0_xattn_b_qkv, L0_xattn_w_ao, L0_xattn_b_ao, L0_xattn_ln2_s, L0_xattn_ln2_b, L0_xattn_w_q, L0_xattn_b_q, L0_xattn_w_kv, L0_xattn_b_kv, L0_xattn_w_co, L0_xattn_b_co, L0_xattn_ln3_s, L0_xattn_ln3_b, L0_xattn_w1, L0_xattn_b1, L0_xattn_w2, L0_xattn_b2):
    import jax
    import jax.numpy as jnp

    def _L0_xattn_ref(hidden_states, encoder_states, ltor_mask, cross_mask, ln1_s, ln1_b, w_qkv, b_qkv, w_ao, b_ao, ln2_s, ln2_b, w_q, b_q, w_kv, b_kv, w_co, b_co, ln3_s, ln3_b, w1, b1, w2, b2):
        import jax, jax.numpy as jnp
        import numpy as np
        H = 512
        NH = 16
        HD = H // NH
        EPS = 1e-05

        def gelu(x):
            return 0.5 * x * (1.0 + jnp.tanh(0.7978845608028654 * x * (1.0 + 0.044715 * x * x)))

        def layernorm(x, scale, bias):
            m = jnp.mean(x, axis=-1, keepdims=True)
            v = jnp.mean(jnp.square(x - m), axis=-1, keepdims=True)
            return (x - m) * jax.lax.rsqrt(v + EPS) * scale + bias

        def split_heads(x):
            b, s, _ = x.shape
            return x.reshape(b, s, NH, HD).transpose(0, 2, 1, 3)

        def merge_heads(x):
            b, nh, s, hd = x.shape
            return x.transpose(0, 2, 1, 3).reshape(b, s, nh * hd)

        def attention(q, k, v, mask):
            scores = jnp.einsum('bhqd,bhkd->bhqk', q, k) / jnp.sqrt(jnp.float32(HD))
            scores = scores * mask - 10000.0 * (1.0 - mask)
            probs = jax.nn.softmax(scores, axis=-1)
            return jnp.einsum('bhqk,bhkd->bhqd', probs, v)
        ln_out = layernorm(hidden_states, ln1_s, ln1_b)
        qkv = ln_out @ w_qkv + b_qkv
        q, k, v = jnp.split(qkv, 3, axis=-1)
        ctx = merge_heads(attention(split_heads(q), split_heads(k), split_heads(v), ltor_mask))
        attn_out = ctx @ w_ao + b_ao
        x = hidden_states + attn_out
        ln_out = layernorm(x, ln2_s, ln2_b)
        q = ln_out @ w_q + b_q
        kv = encoder_states @ w_kv + b_kv
        k, v = jnp.split(kv, 2, axis=-1)
        ctx = merge_heads(attention(split_heads(q), split_heads(k), split_heads(v), cross_mask))
        cross_out = ctx @ w_co + b_co
        x = x + cross_out
        ln_out = layernorm(x, ln3_s, ln3_b)
        mlp_out = gelu(ln_out @ w1 + b1) @ w2 + b2
        return x + mlp_out
    x = _L0_xattn_ref(x, ctx_2048, mask_1x1xSxS2_fc1, mask_Bx1xSxS2_ff1, L0_xattn_ln1_s, L0_xattn_ln1_b, L0_xattn_w_qkv, L0_xattn_b_qkv, L0_xattn_w_ao, L0_xattn_b_ao, L0_xattn_ln2_s, L0_xattn_ln2_b, L0_xattn_w_q, L0_xattn_b_q, L0_xattn_w_kv, L0_xattn_b_kv, L0_xattn_w_co, L0_xattn_b_co, L0_xattn_ln3_s, L0_xattn_ln3_b, L0_xattn_w1, L0_xattn_b1, L0_xattn_w2, L0_xattn_b2)
    return x

_drawn_inputs = setup_inputs


def setup_inputs(seed=0):
    import zlib

    import numpy as np

    out = dict(_drawn_inputs(seed))
    spreads = {'L0_xattn_ln1_s': (1.0, 0.6),
     'L0_xattn_ln1_b': (0.0, 0.403),
     'L0_xattn_b_qkv': (0.0, 0.1),
     'L0_xattn_b_ao': (0.0, 0.1),
     'L0_xattn_ln2_s': (1.0, 0.6),
     'L0_xattn_ln2_b': (0.0, 0.8),
     'L0_xattn_b_q': (0.0, 2.0),
     'L0_xattn_b_kv': (0.0, 0.1),
     'L0_xattn_b_co': (0.0, 0.1),
     'L0_xattn_ln3_s': (1.0, 0.2),
     'L0_xattn_ln3_b': (0.0, 0.325),
     'L0_xattn_b1': (0.0, 0.1),
     'L0_xattn_b2': (0.0, 0.1)}
    factors = {'L0_xattn_w_q': 7.061}
    for name, (base, spread) in spreads.items():
        noise = np.random.default_rng([zlib.crc32(name.encode()), seed]).standard_normal(out[name].shape)
        drawn = base * np.exp(spread * noise) if base else spread * noise
        out[name] = jnp.asarray(drawn.astype(out[name].dtype))
    for name, factor in factors.items():
        out[name] = (out[name] * factor).astype(out[name].dtype)
    return out
```

```python
import math
from contextlib import ExitStack

import concourse.bass as bass
from concourse import mybir
from concourse.alu_op_type import AluOpType as ALU

ACT = mybir.ActivationFunctionType
F32 = mybir.dt.float32
F32R = mybir.dt.float32r
F16 = mybir.dt.float16
BF16 = mybir.dt.bfloat16
AX_X = mybir.AxisListType.X

P = 128
NH = 16
HD = 32
HQ = P // HD
EPS = 1e-5
MASKED = 10000.0
LIFT = 15.0 * math.log(2.0)
VW = 3 * HD + 1
VPAD = VW + 1
HI, LO = 0, 1
PASSES = ((LO, HI), (HI, LO), (HI, HI))


class Looped:

    def __init__(self, register, rate, offset):
        self.register, self.rate, self.offset = register, rate, offset

    def __add__(self, k):
        return Looped(self.register, self.rate, self.offset + k)

    def __sub__(self, k):
        return self + -k

    def __mul__(self, k):
        return Looped(self.register, self.rate * k, self.offset * k)

    __rmul__ = __mul__


def at(x):
    if isinstance(x, Looped):
        assert x.offset >= 0
        return x.register * x.rate + x.offset
    assert x > 0 or isinstance(x, int)
    return x


def xattn_layer(nc, a, out):
    B, S, H = a["x"].shape
    KC = H // P
    F = a["w1"].shape[1]
    FC = F // P
    GB = 2
    NG = B // GB
    NS = KC * GB
    MB = 4
    NM = B // MB
    SCALE = 1.0 / math.sqrt(HD)
    assert S == P and NH * HD == H and KC == 4 and NG >= 4 and NM >= 2

    with ExitStack() as top:
        def sem(name):
            return top.enter_context(nc.semaphore(name))

        def sb(name, shape, dt=F32, where=top):
            return where.enter_context(nc.sbuf_tensor(name, shape, dt))

        def ps(name, shape, dt=F32, where=top):
            return where.enter_context(nc.psum_tensor(name, shape, dt))

        x1_dram = nc.dram_tensor("x_after_self", (B, S, H), F32, kind="Internal").ap()
        x2_dram = nc.dram_tensor("x_after_cross", (B, S, H), F32, kind="Internal").ap()

        ident = sb("ident", [P, P])
        ones = sb("ones", [P, P])
        scale_t = sb("scale_t", [P, P])
        eps_t = sb("eps_t", [P, 1])
        neg_half = sb("neg_half", [P, 1])

        s_const = sem("const_ready")
        with nc.Block() as block:
            @block.gpsimd
            def _(pool):
                nc.gpsimd.memset(ident[:], 0.0).then_inc(s_const, 1)
                nc.gpsimd.memset(ones[:], 1.0).then_inc(s_const, 1)
                nc.gpsimd.memset(scale_t[:], SCALE).then_inc(s_const, 1)
                nc.gpsimd.memset(eps_t[:], EPS).then_inc(s_const, 1)
                nc.gpsimd.memset(neg_half[:], -0.5).then_inc(s_const, 1)
                pool.wait_ge(s_const, 5)
                nc.gpsimd.affine_select(out=ident[:], in_=ident[:], compare_op=ALU.not_equal, fill=1.0,
                                        base=0, pattern=[[-1, P]], channel_multiplier=1).then_inc(s_const, 1)

        w_stage_in = [sem(f"w_stage_in{i}") for i in range(2)]
        w_hi_done, w_lo_done, w_col_done = sem("w_hi_done"), sem("w_lo_done"), sem("w_col_done")
        par_in, par_cols, par_cv = sem("par_in"), sem("par_cols"), sem("par_cv")
        par_row, par_row_ps = sem("par_row"), sem("par_row_ps")
        setup_base = {"unit": 0, "col": 0, "par": 0, "n": 0}

        def load_weights(where, wsp, units, gamma, beta, biases, row_bias, row_unit=None, cv_at=None):
            n = setup_base["n"]
            setup_base["n"] += 1
            U = len(units)
            whi = sb(f"whi{n}", [P, U, KC, H], F32R, wsp)
            wlo = sb(f"wlo{n}", [P, U, KC, H], F32R, wsp)
            ncols = U * KC
            bias_cols = sb(f"bias_cols{n}", [P, ncols], F32, wsp)
            bias_row = sb(f"bias_row{n}", [P, H], F32, wsp)
            with ExitStack() as tmp:
                stage = sb(f"stage{n}", [P, 2, KC, H], F32, tmp)
                g_col = sb(f"g_col{n}", [P, KC], F32, tmp)
                b_col = sb(f"b_col{n}", [P, KC], F32, tmp)
                raw_cols = sb(f"raw_cols{n}", [P, ncols], F32, tmp)
                raw_row = sb(f"raw_row{n}", [1, H], F32, tmp)
                cv = sb(f"cv{n}", [P, KC, P], F32, tmp)
                ps_col = ps(f"ps_col{n}", [P, 512], F32, tmp)
                ps_row = ps(f"ps_row{n}", [P, 512], F32, tmp)
                u0, c0, p0 = setup_base["unit"], setup_base["col"], setup_base["par"]
                normed = [u for u in range(U) if units[u][1]]
                setup_base["unit"] += U
                setup_base["col"] += len(normed)
                loads = 3 + len(biases)
                setup_base["par"] += 16 * loads
                k = n + 1

                with nc.Block() as block:
                    @block.sync
                    def _(sp):
                        for u, (w, _) in enumerate(units):
                            if u >= 2:
                                sp.wait_ge(w_lo_done, u0 + u - 1)
                                if u - 2 in normed:
                                    sp.wait_ge(w_col_done, c0 + normed.index(u - 2) + 1)
                                if u - 2 == row_unit:
                                    sp.wait_ge(par_row_ps, k)
                            i = (u0 + u) % 2
                            sp.dma_start(stage[:, i], w.rearrange("(c p) n -> p c n", p=P)).then_inc(w_stage_in[i], 16)
                            if u == 0:
                                sp.dma_start(g_col[:], gamma.rearrange("(c p) -> p c", p=P),
                                             allow_slow_non_contiguous=True).then_inc(par_in, 16)
                                sp.dma_start(b_col[:], beta.rearrange("(c p) -> p c", p=P),
                                             allow_slow_non_contiguous=True).then_inc(par_in, 16)
                                for vec, at in biases:
                                    m = vec.shape[0] // P
                                    sp.dma_start(raw_cols[:, at:at + m],
                                                 vec.rearrange("(c p) -> p c", p=P),
                                                 allow_slow_non_contiguous=True).then_inc(par_in, 16)
                                sp.dma_start(raw_row[:], row_bias.rearrange("(a n) -> a n", a=1)).then_inc(par_in, 16)

                    @block.scalar
                    def _(act):
                        for u, (_, norm) in enumerate(units):
                            i = (u0 + u) % 2
                            act.wait_ge(w_stage_in[i], 16 * ((u0 + u) // 2 + 1))
                            if u == 0:
                                act.wait_ge(par_in, p0 + 16 * loads)
                            for c in range(KC):
                                last = nc.scalar.activation(whi[:, u, c], stage[:, i, c], ACT.Copy,
                                                            scale=g_col[:, c:c + 1] if norm else 1.0)
                            last.then_inc(w_hi_done, 1)

                    @block.vector
                    def _(dve):
                        for u, (_, norm) in enumerate(units):
                            i = (u0 + u) % 2
                            dve.wait_ge(w_hi_done, u0 + u + 1)
                            for c in range(KC):
                                last = nc.vector.scalar_tensor_tensor(
                                    out=wlo[:, u, c], in0=stage[:, i, c], scalar=g_col[:, c:c + 1] if norm else 1.0,
                                    in1=whi[:, u, c], op0=ALU.mult, op1=ALU.subtract)
                            last.then_inc(w_lo_done, 1)
                            if norm and u == normed[-1]:
                                dve.wait_ge(w_col_done, c0 + len(normed))
                                lo, hi = KC * normed[0], KC * (normed[-1] + 1)
                                end = max(at + vec.shape[0] // P for vec, at in biases)
                                if hi < end:
                                    nc.vector.tensor_copy(bias_cols[:, hi:end], raw_cols[:, hi:end])
                                nc.vector.tensor_tensor(bias_cols[:, lo:hi], ps_col[:, lo:hi], raw_cols[:, lo:hi],
                                                        ALU.add).then_inc(par_cols, 1)
                                if row_unit is not None:
                                    dve.wait_ge(par_cols, k)
                                    for c in range(KC):
                                        last = nc.vector.tensor_scalar(cv[:, c], ones[:],
                                                                       bias_cols[:, cv_at + c:cv_at + c + 1],
                                                                       None, ALU.mult)
                                    last.then_inc(par_cv, 1)
                        dve.wait_ge(par_row_ps, k)
                        nc.vector.tensor_copy(bias_row[:], ps_row[:, 0:H]).then_inc(par_row, 1)

                    @block.tensor
                    def _(pe):
                        pe.wait_ge(par_in, p0 + 16 * loads)
                        for u in normed:
                            i = (u0 + u) % 2
                            pe.wait_ge(w_stage_in[i], 16 * ((u0 + u) // 2 + 1))
                            for m in range(KC):
                                for c in range(KC):
                                    last = nc.tensor.matmul(ps_col[:, KC * u + m:KC * u + m + 1],
                                                            stage[:, i, c, m * P:(m + 1) * P], b_col[:, c:c + 1],
                                                            start=(c == 0), stop=(c == KC - 1))
                            last.then_inc(w_col_done, 1)
                        last = nc.tensor.matmul(ps_row[:, 0:H], ones[0:1, :], raw_row[:], start=True,
                                                stop=row_unit is None)
                        if row_unit is not None:
                            i = (u0 + row_unit) % 2
                            pe.wait_ge(w_stage_in[i], 16 * ((u0 + row_unit) // 2 + 1))
                            pe.wait_ge(par_cv, k)
                            for c in range(KC):
                                last = nc.tensor.matmul(ps_row[:, 0:H], cv[:, c], stage[:, i, c], start=False,
                                                        stop=(c == KC - 1))
                        last.then_inc(par_row_ps, 1)
            return whi, wlo, bias_cols, bias_row

        x_in = [sem(f"x_in{b}") for b in range(GB)]
        enc_in = [sem(f"enc_in{b}") for b in range(GB)]
        mask_in = [sem(f"mask_in{b}") for b in range(GB)]
        res_in = [sem(f"res_in{b}") for b in range(GB)]
        stored = [sem(f"stored{b}") for b in range(GB)]
        kbd_in = [sem(f"kbd_in{i}") for i in range(2)]
        names = ("sc_done pt_done pv_done k_done q_done v_done o_done xT_done encT_done cT_done exp_done pth_done "
                 "kh_done qh_done v1_done v2_done xTh_done encTh_done cTh_done masked mx_done nb_done ptl_done "
                 "kl_done ql_done vr_done xTl_done encTl_done cTl_done stats_done aggr_done rstd_done xn_done "
                 "eps_added sums_done ctx_done y_done biased v3_done mask_ready res_ready kbd_clear ones_ready")
        s = {name: sem(name) for name in names.split()}

        def attention(st, w, g0, cross, x_src, enc_src, mask_src, dst):
            whi, wlo, bias_cols, bias_row = w
            WQ, WK, WV, WO = range(4)
            pre = "c" if cross else "s"

            def buf(name, shape, dt=F32):
                return sb(f"{pre}_{name}", shape, dt, st)

            x_t = buf("x_t", [P, GB, H])
            xn = buf("xn", [P, GB, H])
            enc_t = buf("enc_t", [P, GB, H]) if cross else None
            res_t = buf("res_t", [P, GB, H])
            y_t = buf("y_t", [P, GB, H])
            m_raw = buf("m_raw", [P, GB, P])
            m_mul = buf("m_mul", [P, GB, P])
            m_add = buf("m_add", [P, GB, P])
            xT = buf("xT", [P, 2, KC, GB * P], F32R)
            encT = buf("encT", [P, 2, KC, GB * P], F32R) if cross else xT
            q_r = buf("q_r", [P, 2, 2, GB * P], F32R)
            k_r = buf("k_r", [P, 2, 2, GB * P], F32R)
            k_bd = buf("k_bd", [P, 2, 2, GB, HQ * P], F32R)
            v_b = buf("v_b", [P, GB, NH, VPAD], BF16)
            v_rest = buf("v_rest", [P, GB, H])
            t_s = buf("t_s", [P, 2, HQ, P])
            p_s = buf("p_s", [P, 2, HQ, P])
            mx = buf("mx", [P, 2, HQ])
            nb = buf("nb", [P, 2, HQ])
            pT = buf("pT", [P, 2, 2, HQ * P], F16)
            csum = buf("csum", [P, 2, HQ, HD])
            rcp = buf("rcp", [P, 2, HQ])
            ctx_t = buf("ctx_t", [P, GB, H])
            cT = buf("cT", [P, GB, 2, KC, P], F32R)
            stat = buf("stat", [P, GB, 6])
            mv = buf("mv", [P, GB, 2])
            rstd = buf("rstd", [P, GB, 1])

            ps_s = [ps(f"{pre}_ps_s{i}", [P, HQ, P], F32, st) for i in range(2)]
            ps_t = [ps(f"{pre}_ps_t{i}", [P, HQ, P], F32, st) for i in range(2)]
            ps_p = [ps(f"{pre}_ps_p{i}", [P, H], F32, st) for i in range(2)]
            ps_o = ps(f"{pre}_ps_o", [P, HQ, P], F32, st)
            ps_x = ps(f"{pre}_ps_x", [P, KC, P], F32, st)

            gN = g0 + NG

            def lag(g, n, by):
                return (g, n - by) if n >= by else (g - 1, n - by + NS)

            def slot_no(g, n):
                return g * NS + n + 1

            def live(g, cur, prev):
                return lambda gg: (cur if gg is g else prev)

            def run(engine, slot):
                for n in range(4, NS):
                    slot(g0 - 1, n, False, False, True)
                for n in range(NS):
                    slot(g0, n, True, False, True)
                for n in range(NS):
                    slot(g0 + 1, n, True, True, True)
                with engine.Fori(0, NG - 3) as i:
                    g = Looped(i, 1, g0 + 2)
                    for n in range(NS):
                        slot(g, n, True, True, True)
                for n in range(NS):
                    slot(gN - 1, n, True, True, False)
                for n in range(6):
                    slot(gN, n, False, True, False)

            def known(g, least):
                return not isinstance(g, int) or g >= least

            with nc.Block() as block:
                @block.sync
                def _(sp):
                    def load_x(g, b):
                        if known(g, g0 + 1):
                            sp.wait_ge(s["xn_done"], at(g * GB - GB + b + 1))
                        sp.dma_start(x_t[:, b], x_src[row(g, b)]).then_inc(x_in[b], 16)

                    def row(g, b):
                        r = (g - g0) * GB + b
                        return r if isinstance(r, int) else bass.ds(at(r), 1)

                    def load_enc(g, b):
                        if known(g, g0 + 1):
                            sp.wait_ge(s["encT_done"], at((g - g0) * GB - GB + b + 1))
                        sp.dma_start(enc_t[:, b], enc_src[row(g, b)]).then_inc(enc_in[b], 16)

                    def load_mask(g, b):
                        if known(g, g0 + 1):
                            sp.wait_ge(s["mask_ready"], at(2 * ((g - 1) * GB + b + 1)))
                        src = mask_src[row(g, b), 0] if cross else mask_src[0, 0]
                        sp.dma_start(m_raw[:, b], src).then_inc(mask_in[b], 16)

                    def load_res(g, b):
                        if known(g, g0 + 1):
                            sp.wait_ge(s["y_done"], at((g - 1) * GB + b + 1))
                        sp.dma_start(res_t[:, b], x_src[row(g, b)]).then_inc(res_in[b], 16)

                    def place_k(g, c):
                        i = c % 2
                        if known(g, g0):
                            sp.wait_ge(s["kl_done"], at(g * KC + c + 1))
                        if c < 2 and not known(g, g0 + 1):
                            sp.wait_ge(s["kbd_clear"], at(1 + cross))
                        for j in range(HQ):
                            r = slice(HD * j, HD * (j + 1))
                            sp.dma_start(
                                k_bd[r, i, :, :, P * j:P * (j + 1)].rearrange("p h b t -> p (h b) t").bitcast(F32),
                                k_r[r, i].rearrange("p h (b t) -> p (h b) t", b=GB).bitcast(F32)
                                ).then_inc(kbd_in[i], 16)

                    def slot(g, n, cur, prev, nxt):
                        if n == 0 and cur and nxt:
                            load_x(g + 1, 0)
                            load_x(g + 1, 1)
                        if n in (1, 3) and cur:
                            place_k(g, (n + 3) // 2)
                        if n == 1 and cur and nxt and cross:
                            load_enc(g + 1, 0)
                            load_enc(g + 1, 1)
                        if n == 3 and cur and nxt:
                            load_mask(g + 1, 0)
                            load_mask(g + 1, 1)
                        if n in (5, 6) and prev:
                            store(g - 1, n - 5)
                        if n in (5, 7) and nxt:
                            place_k(g + 1, (n - 5) // 2)
                        if n in (6, 7) and cur:
                            load_res(g, n - 6)

                    def store(g, b):
                        sp.wait_ge(s["y_done"], at(g * GB + b + 1))
                        sp.dma_start(dst[row(g, b)], y_t[:, b]).then_inc(stored[b], 16)

                    for b in range(GB):
                        load_x(g0, b)
                        if cross:
                            load_enc(g0, b)
                        load_mask(g0, b)
                    run(sp, slot)
                    store(gN - 1, 1)
                    for b in range(GB):
                        sp.wait_ge(stored[b], at(16 * gN))

                @block.tensor
                def _(pe):
                    def scores(g, n):
                        c, b = divmod(n, GB)
                        i = c % 2
                        pe.wait_ge(kbd_in[i], at(g * (16 * HQ * KC // 2) + 16 * HQ * (c // 2 + 1)))
                        pe.wait_ge(s["ql_done"], at(g * KC + c + 1))
                        if n >= 2 or known(g, g0 + 1):
                            pe.wait_ge(s["masked"], at(slot_no(*lag(g, n, 2))))
                        for x, (hq, hk) in enumerate(PASSES):
                            last = nc.tensor.matmul(ps_s[n % 2][:], q_r[:, i, hq, b * P:(b + 1) * P],
                                                    k_bd[:, i, hk, b], start=(x == 0), stop=(x == 2))
                        last.then_inc(s["sc_done"], 1)

                    def transpose_probs(g, n):
                        pe.wait_ge(s["exp_done"], at(slot_no(g, n)))
                        if n >= 2 or known(g, g0 + 1):
                            pe.wait_ge(s["ptl_done"], at(slot_no(*lag(g, n, 2))))
                        for j in range(HQ):
                            last = nc.tensor.transpose(ps_t[n % 2][:, j], p_s[:, n % 2, j], ident[:])
                        last.then_inc(s["pt_done"], 1)

                    def weigh_values(g, n):
                        c, b = divmod(n, GB)
                        pe.wait_ge(s["ptl_done"], at(slot_no(g, n)))
                        if c == 0:
                            pe.wait_ge(s["v3_done"], at(g * GB + b + 1))
                        if n >= 1 or known(g, g0 + 1):
                            pe.wait_ge(s["sums_done"], at(2 * slot_no(*lag(g, n, 1))))
                        for j in range(HQ):
                            for h in (HI, LO):
                                last = nc.tensor.matmul(ps_o[:, j, 0:VW], pT[:, n % 2, h, j * P:(j + 1) * P],
                                                        v_b[:, b, HQ * c + j, 0:VW], start=(h == HI), stop=(h == LO))
                        last.then_inc(s["pv_done"], 1)

                    def columns(unit, bank, xt, c, done):
                        k = 0
                        for hw, hx in PASSES:
                            for kc in range(KC):
                                last = nc.tensor.matmul(ps_p[bank][:, 0:GB * P],
                                                        (whi, wlo)[hw][:, unit, kc, c * P:(c + 1) * P],
                                                        xt[:, hx, kc], start=(k == 0), stop=(k == 3 * KC - 1))
                                k += 1
                        last.then_inc(s[done], 1)

                    def rows(unit, bank, lhs, done):
                        k = 0
                        for hx, hw in PASSES:
                            for kc in range(KC):
                                last = nc.tensor.matmul(ps_p[bank][:, :], lhs(hx, kc), (whi, wlo)[hw][:, unit, kc],
                                                        start=(k == 0), stop=(k == 3 * KC - 1))
                                k += 1
                        last.then_inc(s[done], 1)

                    def keys(g, c, prev):
                        if c == 0:
                            if cross:
                                pe.wait_ge(s["encTl_done"], at((g - g0 + 1) * GB))
                            else:
                                pe.wait_ge(s["xTl_done"], at((g + 1) * GB))
                            if prev:
                                pe.wait_ge(s["y_done"], at((g - 2) * GB + 1))
                            elif known(g, g0 + 1):
                                pe.wait_ge(s["kl_done"], at(g * KC))
                        elif c == 3:
                            pe.wait_ge(s["vr_done"], at(g * GB + 2))
                        else:
                            pe.wait_ge(s["kl_done"], at(g * KC + c))
                        columns(WK, 0, encT, c, "k_done")

                    def queries(g, c, prev):
                        if c == 0:
                            pe.wait_ge(s["xTl_done"], at((g + 1) * GB))
                            if prev:
                                pe.wait_ge(s["y_done"], at((g - 1) * GB))
                            elif known(g, g0 + 1):
                                pe.wait_ge(s["ql_done"], at(g * KC))
                        elif c == 2:
                            pe.wait_ge(s["vr_done"], at(g * GB + 1))
                        else:
                            pe.wait_ge(s["ql_done"], at(g * KC + c))
                        columns(WQ, 1, xT, c, "q_done")

                    def values(g, b):
                        pe.wait_ge(s["ql_done" if b == 0 else "kl_done"], at(g * KC + 2 + b))
                        rows(WV, 1 - b, lambda h, kc: encT[:, h, kc, b * P:(b + 1) * P], "v_done")

                    def outputs(g, b, cur):
                        pe.wait_ge(s["cTl_done"], at(g * GB + b + 1))
                        last = (g + 1) * KC + (KC if cur else 0)
                        pe.wait_ge(s["kl_done" if b == 0 else "ql_done"], at(last))
                        rows(WO, b, lambda h, kc: cT[:, b, h, kc], "o_done")

                    def flip(src, b, done):
                        for kc in range(KC):
                            last = nc.tensor.transpose(ps_x[:, kc], src[:, b, kc * P:(kc + 1) * P], ident[:])
                        last.then_inc(s[done], 1)

                    def flip_ctx(g, b):
                        pe.wait_ge(s["ctx_done"], at(slot_no(g, NS - GB + b)))
                        if b == 0:
                            if known(g, g0 + NG - 1):
                                pe.wait_ge(s["xTl_done"], at((g + 1) * GB))
                            else:
                                pe.wait_ge(s["xTl_done"], at((g + 2) * GB))
                        else:
                            pe.wait_ge(s["cTl_done"], at(g * GB + b))
                        flip(ctx_t, b, "cT_done")

                    def flip_x(g, b):
                        pe.wait_ge(s["xn_done"], at(g * GB + b + 1))
                        if b == 1:
                            pe.wait_ge(s["xTl_done"], at(g * GB + b))
                        elif cross:
                            pe.wait_ge(s["encTl_done"], at((g - g0) * GB + 2))
                        elif known(g, g0 + 2):
                            pe.wait_ge(s["cTl_done"], at((g - 1) * GB))
                        elif known(g, g0 + 1):
                            pe.wait_ge(s["xTl_done"], at(g * GB))
                        flip(xn, b, "xT_done")

                    def flip_enc(g, b):
                        pe.wait_ge(enc_in[b], at(16 * (g - g0 + 1)))
                        if b == 1:
                            pe.wait_ge(s["encTl_done"], at((g - g0) * GB + b))
                        elif known(g, g0 + 2):
                            pe.wait_ge(s["cTl_done"], at((g - 1) * GB))
                        elif known(g, g0 + 1):
                            pe.wait_ge(s["xTl_done"], at(g * GB))
                        flip(enc_t, b, "encT_done")

                    def slot(g, n, cur, prev, nxt):
                        if cur:
                            scores(g, n)
                        gt, nt = lag(g, n, 2)
                        if cur if n >= 2 else prev:
                            transpose_probs(gt, nt)
                        if n in (3, 4) and prev:
                            flip_ctx(g - 1, n - 3)
                        if n < 5 and cur:
                            (queries if n % 2 == 0 else keys)(g, (n + 2) // 2 if n % 2 == 0 else (n + 3) // 2, prev)
                        if n == 6 and nxt and cross:
                            flip_x(g + 1, 1)
                        if n == 7 and nxt:
                            keys(g + 1, 1, prev)
                        gv, nv = lag(g, n, 3)
                        if cur if n >= 3 else prev:
                            weigh_values(gv, nv)
                        if n in (1, 2) and cur:
                            values(g, n - 1)
                        if n == 5 and nxt:
                            (flip_enc if cross else flip_x)(g + 1, 1)
                        if n in (4, 5) and prev:
                            outputs(g - 1, n - 4, cur)
                        if n == 4 and nxt:
                            (flip_enc if cross else flip_x)(g + 1, 0)
                        if n == 5 and nxt:
                            if cross:
                                flip_x(g + 1, 0)
                            keys(g + 1, 0, prev)
                        if n == 6 and nxt:
                            queries(g + 1, 0, prev)

                    pe.wait_ge(s_const, 6)
                    run(pe, slot)

                @block.scalar
                def _(act):
                    def high_probs(g, n):
                        act.wait_ge(s["pt_done"], at(slot_no(g, n)))
                        if n >= 2 or known(g, g0 + 1):
                            act.wait_ge(s["pv_done"], at(slot_no(*lag(g, n, 2))))
                        nc.scalar.copy(pT[:, n % 2, HI], ps_t[n % 2][:].rearrange("p j t -> p (j t)")
                                       ).then_inc(s["pth_done"], 1)

                    def exponent(g, n):
                        act.wait_ge(s["nb_done"], at(slot_no(g, n)))
                        if n >= 2 or known(g, g0 + 1):
                            act.wait_ge(s["pt_done"], at(slot_no(*lag(g, n, 2))))
                        for j in range(HQ):
                            last = nc.scalar.activation(p_s[:, n % 2, j], t_s[:, n % 2, j], ACT.Exp,
                                                        bias=nb[:, n % 2, j:j + 1])
                        last.then_inc(s["exp_done"], 1)

                    def high_cols(g, c, unit, bank, dst_t, done, high):
                        act.wait_ge(s[done], at(g * KC + c + 1))
                        i = c % 2
                        if c >= 2:
                            act.wait_ge(s["sc_done"], at(slot_no(g, (c - 1) * GB - 1)))
                        elif known(g, g0 + 1):
                            act.wait_ge(s["sc_done"], at(slot_no(g - 1, (c + KC - 1) * GB - 1)))
                        if unit == WK:
                            if c >= 2 or known(g, g0 + 1):
                                act.wait_ge(kbd_in[i], at(g * (16 * HQ * KC // 2) + 16 * HQ * (c // 2)))
                        nc.scalar.activation(dst_t[:, i, HI], ps_p[bank][:, 0:GB * P], ACT.Identity,
                                             bias=bias_cols[:, KC * unit + c:KC * unit + c + 1]
                                             ).then_inc(s[high], 1)

                    def value_top(g, b):
                        act.wait_ge(s["v_done"], at(g * GB + b + 1))
                        if known(g, g0 + 1):
                            act.wait_ge(s["pv_done"], at(slot_no(g - 1, NS - GB + b)))
                        else:
                            act.wait_ge(s["ones_ready"], at(1 + cross))
                        nc.scalar.copy(v_b[:, b, :, 0:HD], ps_p[1 - b][:].rearrange("p (h d) -> p h d", h=NH)
                                       ).then_inc(s["v1_done"], 1)

                    def value_middle(g, b):
                        act.wait_ge(s["vr_done"], at(g * GB + b + 1))
                        nc.scalar.copy(v_b[:, b, :, HD:2 * HD], v_rest[:, b].rearrange("p (h d) -> p h d", h=NH)
                                       ).then_inc(s["v2_done"], 1)

                    def high_flip(dst_t, done, count, free, high):
                        act.wait_ge(s[done], at(count))
                        for name, value in free:
                            act.wait_ge(s[name], at(value))
                        nc.scalar.copy(dst_t, ps_x[:]).then_inc(s[high], 1)

                    def flip_x(g, b):
                        free = [("q_done", g * KC)] if known(g, g0 + 1) else []
                        if free and not cross:
                            free.append(("v_done", g * GB))
                        high_flip(xT[:, HI, :, b * P:(b + 1) * P], "xT_done", g * GB + b + 1, free, "xTh_done")

                    def flip_enc(g, b):
                        free = [("k_done", g * KC)] if known(g, g0 + 1) else []
                        high_flip(encT[:, HI, :, b * P:(b + 1) * P], "encT_done", (g - g0) * GB + b + 1, free,
                                  "encTh_done")

                    def flip_ctx(g, b):
                        free = [("o_done", (g - 1) * GB + b + 1)] if known(g, g0 + 1) else []
                        high_flip(cT[:, b, HI], "cT_done", g * GB + b + 1, free, "cTh_done")

                    def slot(g, n, cur, prev, nxt):
                        gt, nt = lag(g, n, 2)
                        if cur if n >= 2 else prev:
                            high_probs(gt, nt)
                        if n in (3, 4) and prev:
                            flip_ctx(g - 1, n - 3)
                        ge, ne = lag(g, n, 1)
                        if cur if n >= 1 else prev:
                            exponent(ge, ne)
                        if n in (2, 3) and cur:
                            value_middle(g, n - 2)
                        if n in (0, 2, 4) and cur:
                            high_cols(g, n // 2 + 1, WQ, 1, q_r, "q_done", "qh_done")
                        if n in (1, 3) and cur:
                            high_cols(g, (n + 3) // 2, WK, 0, k_r, "k_done", "kh_done")
                        if n == 6 and nxt and cross:
                            flip_x(g + 1, 1)
                        if n == 7 and nxt:
                            high_cols(g + 1, 1, WK, 0, k_r, "k_done", "kh_done")
                        if n in (1, 2) and cur:
                            value_top(g, n - 1)
                        if n == 4 and nxt:
                            (flip_enc if cross else flip_x)(g + 1, 0)
                        if n == 5 and nxt:
                            (flip_enc if cross else flip_x)(g + 1, 1)
                            if cross:
                                flip_x(g + 1, 0)
                            high_cols(g + 1, 0, WK, 0, k_r, "k_done", "kh_done")
                        if n == 6 and nxt:
                            high_cols(g + 1, 0, WQ, 1, q_r, "q_done", "qh_done")

                    run(act, slot)

                @block.vector
                def _(dve):
                    def mask_scores(g, n):
                        b = n % GB
                        dve.wait_ge(s["sc_done"], at(slot_no(g, n)))
                        if n < GB:
                            dve.wait_ge(s["mask_ready"], at(2 * (g * GB + b + 1)))
                        if n >= 2 or known(g, g0 + 1):
                            dve.wait_ge(s["exp_done"], at(slot_no(*lag(g, n, 2))))
                        nc.vector.tensor_tensor(t_s[:, n % 2], ps_s[n % 2][:],
                                                m_mul[:, b].unsqueeze(1).to_broadcast([P, HQ, P]),
                                                ALU.mult).then_inc(s["masked"], 1)

                    def low_probs(g, n):
                        dve.wait_ge(s["pth_done"], at(slot_no(g, n)))
                        nc.vector.tensor_tensor(pT[:, n % 2, LO], ps_t[n % 2][:].rearrange("p j t -> p (j t)"),
                                                pT[:, n % 2, HI], ALU.subtract).then_inc(s["ptl_done"], 1)

                    def maxima(g, n, stats):
                        if stats is not None:
                            dve.wait_ge(s["stats_done"], at(stats))
                        dve.wait_ge(s["biased"], at(slot_no(g, n)))
                        nc.vector.tensor_reduce(mx[:, n % 2], t_s[:, n % 2], AX_X, ALU.max).then_inc(s["mx_done"], 1)
                        dve.wait_ge(s["mx_done"], at(slot_no(g, n)))
                        nc.vector.tensor_scalar(nb[:, n % 2], mx[:, n % 2], -1.0, LIFT, ALU.mult,
                                                ALU.add).then_inc(s["nb_done"], 1)

                    def context(g, n):
                        c, b = divmod(n, GB)
                        dve.wait_ge(s["pv_done"], at(slot_no(g, n)))
                        if n >= 2 or known(g, g0 + 1):
                            dve.wait_ge(s["ctx_done"], at(slot_no(*lag(g, n, 2))))
                        nc.vector.tensor_reduce(csum[:, n % 2], ps_o[:, :, 0:3 * HD].rearrange(
                            "p j (t d) -> p j d t", t=3), AX_X, ALU.add).then_inc(s["sums_done"], 1)
                        nc.vector.reciprocal(rcp[:, n % 2], ps_o[:, :, 3 * HD]).then_inc(s["sums_done"], 1)
                        dve.wait_ge(s["sums_done"], at(2 * slot_no(g, n)))
                        if c == 0 and known(g, g0 + 1):
                            dve.wait_ge(s["cT_done"], at((g - 1) * GB + b + 1))
                        nc.vector.tensor_tensor(ctx_t[:, b, c * P:(c + 1) * P].rearrange("p (j d) -> p j d", j=HQ),
                                                csum[:, n % 2],
                                                rcp[:, n % 2].unsqueeze(2).to_broadcast([P, HQ, HD]),
                                                ALU.mult).then_inc(s["ctx_done"], 1)

                    def low_cols(g, c, unit, bank, dst_t, high, low):
                        dve.wait_ge(s[high], at(g * KC + c + 1))
                        i = c % 2
                        nc.vector.scalar_tensor_tensor(
                            out=dst_t[:, i, LO], in0=ps_p[bank][:, 0:GB * P],
                            scalar=bias_cols[:, KC * unit + c:KC * unit + c + 1], in1=dst_t[:, i, HI],
                            op0=ALU.add, op1=ALU.subtract).then_inc(s[low], 1)

                    def value_rest(g, b):
                        dve.wait_ge(s["v1_done"], at(g * GB + b + 1))
                        if known(g, g0 + 1):
                            dve.wait_ge(s["v3_done"], at(g * GB + b - 1))
                        nc.vector.tensor_tensor(v_rest[:, b].rearrange("p (h d) -> p h d", h=NH),
                                                ps_p[1 - b][:].rearrange("p (h d) -> p h d", h=NH),
                                                v_b[:, b, :, 0:HD], ALU.subtract).then_inc(s["vr_done"], 1)

                    def low_flip(hi_t, lo_t, high, count, low):
                        dve.wait_ge(s[high], at(count))
                        nc.vector.tensor_tensor(lo_t, ps_x[:], hi_t, ALU.subtract).then_inc(s[low], 1)

                    def flip_x(g, b):
                        cols = slice(b * P, (b + 1) * P)
                        low_flip(xT[:, HI, :, cols], xT[:, LO, :, cols], "xTh_done", g * GB + b + 1, "xTl_done")

                    def flip_enc(g, b):
                        cols = slice(b * P, (b + 1) * P)
                        low_flip(encT[:, HI, :, cols], encT[:, LO, :, cols], "encTh_done", (g - g0) * GB + b + 1,
                                 "encTl_done")

                    def flip_ctx(g, b):
                        low_flip(cT[:, b, HI], cT[:, b, LO], "cTh_done", g * GB + b + 1, "cTl_done")

                    def statistics(g, b):
                        dve.wait_ge(x_in[b], at(16 * (g + 1)))
                        nc.vector.bn_stats(stat[:, b], x_t[:, b]).then_inc(s["stats_done"], 1)

                    def moments(g, b):
                        nc.vector.bn_aggr(mv[:, b], stat[:, b]).then_inc(s["aggr_done"], 1)

                    def norm(g, b):
                        k = g * GB + b + 1
                        dve.wait_ge(s["rstd_done"], at(k))
                        if known(g, g0 + 1):
                            dve.wait_ge(s["xT_done"], at(k - GB))
                        nc.vector.tensor_scalar(xn[:, b], x_t[:, b], mv[:, b, 0:1], rstd[:, b], ALU.subtract,
                                                ALU.mult).then_inc(s["xn_done"], 1)

                    def output_row(g, b):
                        k = g * GB + b + 1
                        dve.wait_ge(s["o_done"], at(k))
                        dve.wait_ge(s["res_ready"], at(k))
                        if known(g, g0 + 1):
                            dve.wait_ge(stored[b], at(16 * g))
                        nc.vector.tensor_tensor(y_t[:, b], ps_p[b][:], res_t[:, b],
                                                ALU.add).then_inc(s["y_done"], 1)

                    def slot(g, n, cur, prev, nxt):
                        normed = n in (1, 2) and cur and nxt
                        if normed:
                            statistics(g + 1, n - 1)
                        gm, nm = lag(g, n, 1)
                        if cur if n >= 1 else prev:
                            maxima(gm, nm, (g + 1) * GB + n if normed else None)
                        if cur:
                            mask_scores(g, n)
                        if n in (3, 4) and prev:
                            flip_ctx(g - 1, n - 3)
                        gt, nt = lag(g, n, 2)
                        if cur if n >= 2 else prev:
                            low_probs(gt, nt)
                        if n in (0, 2, 4) and cur:
                            low_cols(g, n // 2 + 1, WQ, 1, q_r, "qh_done", "ql_done")
                        if n in (1, 3) and cur:
                            low_cols(g, (n + 3) // 2, WK, 0, k_r, "kh_done", "kl_done")
                        if n == 6 and nxt and cross:
                            flip_x(g + 1, 1)
                        if n == 7 and nxt:
                            low_cols(g + 1, 1, WK, 0, k_r, "kh_done", "kl_done")
                        gv, nv = lag(g, n, 3)
                        if cur if n >= 3 else prev:
                            context(gv, nv)
                        if normed:
                            moments(g + 1, n - 1)
                        if n in (1, 2) and cur:
                            value_rest(g, n - 1)
                        if n == 5 and nxt:
                            (flip_enc if cross else flip_x)(g + 1, 1)
                        if n in (4, 5) and prev:
                            output_row(g - 1, n - 4)
                        if n == 4 and nxt:
                            (flip_enc if cross else flip_x)(g + 1, 0)
                        if n == 5 and nxt:
                            if cross:
                                flip_x(g + 1, 0)
                            low_cols(g + 1, 0, WK, 0, k_r, "kh_done", "kl_done")
                        if n == 6 and nxt:
                            low_cols(g + 1, 0, WQ, 1, q_r, "qh_done", "ql_done")
                        if n in (2, 3) and cur and nxt:
                            norm(g + 1, n - 2)

                    for b in range(GB):
                        statistics(g0, b)
                        dve.wait_ge(s["stats_done"], g0 * GB + b + 1)
                        moments(g0, b)
                        norm(g0, b)
                    run(dve, slot)

                @block.gpsimd
                def _(pool):
                    def root(g, b):
                        pool.wait_ge(s["aggr_done"], at(g * GB + b + 1))
                        nc.gpsimd.tensor_tensor(rstd[:, b], mv[:, b, 1:2], eps_t[:], ALU.add).then_inc(s["eps_added"], 1)
                        pool.wait_ge(s["eps_added"], at(g * GB + b + 1))
                        nc.gpsimd.tensor_tensor(rstd[:, b], rstd[:, b], neg_half[:], ALU.pow
                                                ).then_inc(s["rstd_done"], 1)

                    def prepare_mask(g, b):
                        k = 2 * (g * GB + b)
                        pool.wait_ge(mask_in[b], at(16 * (g + 1)))
                        if known(g, g0 + 1):
                            pool.wait_ge(s["biased"], at(slot_no(g - 1, NS - GB + b)))
                        nc.gpsimd.tensor_tensor(m_mul[:, b], m_raw[:, b], scale_t[:],
                                                ALU.mult).then_inc(s["mask_ready"], 1)
                        nc.gpsimd.tensor_scalar(m_add[:, b], m_raw[:, b], MASKED, -MASKED, ALU.mult,
                                                ALU.add).then_inc(s["mask_ready"], 1)

                    def add_bias(g, n):
                        b = n % GB
                        pool.wait_ge(s["masked"], at(slot_no(g, n)))
                        if n < GB:
                            pool.wait_ge(s["mask_ready"], at(2 * (g * GB + b + 1)))
                        nc.gpsimd.tensor_tensor(t_s[:, n % 2], t_s[:, n % 2],
                                                m_add[:, b].unsqueeze(1).to_broadcast([P, HQ, P]),
                                                ALU.add).then_inc(s["biased"], 1)

                    def value_last(g, b):
                        pool.wait_ge(s["v2_done"], at(g * GB + b + 1))
                        nc.gpsimd.tensor_tensor(v_b[:, b, :, 2 * HD:3 * HD],
                                                v_rest[:, b].rearrange("p (h d) -> p h d", h=NH),
                                                v_b[:, b, :, HD:2 * HD], ALU.subtract).then_inc(s["v3_done"], 1)

                    def residual(g, b):
                        pool.wait_ge(res_in[b], at(16 * (g + 1)))
                        nc.gpsimd.tensor_tensor(res_t[:, b], res_t[:, b], bias_row[:],
                                                ALU.add).then_inc(s["res_ready"], 1)

                    def slot(g, n, cur, prev, nxt):
                        if n in (2, 3) and cur and nxt:
                            root(g + 1, n - 2)
                        if n == 0 and cur:
                            prepare_mask(g, 1)
                        if n == 7 and nxt:
                            prepare_mask(g + 1, 0)
                        if cur:
                            add_bias(g, n)
                        if n in (2, 3) and cur:
                            value_last(g, n - 2)
                        if n in (0, 1) and prev:
                            residual(g - 1, n)

                    for b in range(GB):
                        last = nc.gpsimd.memset(v_b[:, b, :, 3 * HD:VPAD], 1.0)
                    last.then_inc(s["ones_ready"], 1)
                    nc.gpsimd.memset(k_bd[:].rearrange("p i h b t -> p (i h b t)").bitcast(F32),
                                     0.0).then_inc(s["kbd_clear"], 1)
                    pool.wait_ge(s["kbd_clear"], at(1 + cross))
                    root(g0, 0)
                    root(g0, 1)
                    run(pool, slot)

        m_x_in = [sem(f"m_x_in{b}") for b in range(MB)]
        m_res_in = [sem(f"m_res_in{b}") for b in range(MB)]
        m_stored = [sem(f"m_stored{b}") for b in range(MB)]
        m_names = ("h_done gelu_done gh_done gl_done down_done m_xT_done m_xTh_done m_xTl_done m_stats_done "
                   "m_aggr_done m_eps_added m_rstd_done m_xn_done m_y_done m_res_ready")
        m = {name: sem(name) for name in m_names.split()}

        def mlp(st, w, x_src, dst):
            whi, wlo, bias_cols, bias_row = w
            LAG = 2
            TF = MB * P
            x_t = sb("m_x_t", [P, 2, H], F32, st)
            xn = sb("m_xn", [P, MB, H], F32, st)
            xT = sb("m_xT", [P, 2, KC, TF], F32R, st)
            res_t = sb("m_res_t", [P, MB, H], F32, st)
            g_t = sb("m_g_t", [P, 2, TF], F32, st)
            g_r = sb("m_g_r", [P, 2, 2, TF], F32R, st)
            stat = sb("m_stat", [P, MB, 6], F32, st)
            mv = sb("m_mv", [P, MB, 2], F32, st)
            rstd = sb("m_rstd", [P, MB, 1], F32, st)
            ps_h = [ps(f"m_ps_h{i}", [P, TF], F32, st) for i in range(2)]
            ps_x = [ps(f"m_ps_x{i}", [P, KC, P], F32, st) for i in range(2)]
            ps_y = [ps(f"m_ps_y{i}", [P, H], F32, st) for i in range(MB)]

            def known(g, least):
                return not isinstance(g, int) or g >= least

            def run(engine, steps):
                steps(-1, False, False, True)
                steps(0, True, False, True)
                if NM > 2:
                    with engine.Fori(0, NM - 2) as i:
                        steps(Looped(i, 1, 1), True, True, True)
                steps(NM - 1, True, True, False)

            def row(g, b):
                r = g * MB + b
                return r if isinstance(r, int) else bass.ds(at(r), 1)

            with nc.Block() as block:
                @block.sync
                def _(sp):
                    def load_x(g, b):
                        if b >= 2 or known(g, 1):
                            sp.wait_ge(m["m_xn_done"], at(g * MB + b - 1))
                        sp.dma_start(x_t[:, b % 2], x_src[row(g, b)]).then_inc(m_x_in[b], 16)

                    def load_res(g, b):
                        if known(g, 1):
                            sp.wait_ge(m_stored[b], at(16 * g))
                        sp.dma_start(res_t[:, b], x_src[row(g, b)]).then_inc(m_res_in[b], 16)

                    def store(g, b):
                        sp.wait_ge(m["m_y_done"], at(g * MB + b + 1))
                        sp.dma_start(dst[row(g, b)], res_t[:, b]).then_inc(m_stored[b], 16)

                    def steps(g, cur, prev, nxt):
                        if cur and prev:
                            for b in range(MB):
                                store(g - 1, b)
                        if cur:
                            for b in range(MB):
                                load_res(g, b)
                        if nxt:
                            for b in range(MB):
                                load_x(g + 1, b)

                    run(sp, steps)
                    for b in range(MB):
                        store(NM - 1, b)
                    for b in range(MB):
                        sp.wait_ge(m_stored[b], at(16 * NM))

                @block.tensor
                def _(pe):
                    def up(g, j):
                        if j == 0:
                            pe.wait_ge(m["m_xTl_done"], at((g + 1) * MB))
                        if j >= 2 or known(g, 1):
                            pe.wait_ge(m["gelu_done"], at(g * FC + j - 1))
                        k = 0
                        for hw, hx in PASSES:
                            for kc in range(KC):
                                last = nc.tensor.matmul(
                                    ps_h[j % 2][:], (whi, wlo)[hw][:, j // KC, kc, (j % KC) * P:(j % KC + 1) * P],
                                    xT[:, hx, kc], start=(k == 0), stop=(k == 3 * KC - 1))
                                k += 1
                        last.then_inc(m["h_done"], 1)

                    def down(g, j, b):
                        if b == 0:
                            pe.wait_ge(m["gl_done"], at(g * FC + j + 1))
                        if j == 0 and known(g, 1):
                            pe.wait_ge(m["m_y_done"], at((g - 1) * MB + b + 1))
                        for x, (hg, hw) in enumerate(PASSES):
                            last = nc.tensor.matmul(ps_y[b][:], g_r[:, j % 2, hg, b * P:(b + 1) * P],
                                                    (whi, wlo)[hw][:, KC + j // KC, j % KC],
                                                    start=(j == 0 and x == 0), stop=(j == FC - 1 and x == 2))
                        if b == MB - 1 or j == FC - 1:
                            last.then_inc(m["down_done"], 1)

                    def flip(g, b):
                        pe.wait_ge(m["m_xn_done"], at(g * MB + b + 1))
                        if b >= 2 or known(g, 1):
                            pe.wait_ge(m["m_xTl_done"], at(g * MB + b - 1))
                        for kc in range(KC):
                            last = nc.tensor.transpose(ps_x[b % 2][:, kc], xn[:, b, kc * P:(kc + 1) * P], ident[:])
                        last.then_inc(m["m_xT_done"], 1)

                    def steps(g, cur, prev, nxt):
                        if not cur:
                            for b in range(MB):
                                flip(g + 1, b)
                            return
                        for j in range(FC):
                            up(g, j)
                            if j >= LAG:
                                for b in range(MB):
                                    down(g, j - LAG, b)
                            if j >= FC - 2 and nxt:
                                flip(g + 1, j - FC + 2)
                        for b in range(MB):
                            down(g, FC - 2, b)
                            if b == 1 and nxt:
                                flip(g + 1, 2)
                        for b in range(MB):
                            if b == 1 and nxt:
                                flip(g + 1, 3)
                            down(g, FC - 1, b)

                    run(pe, steps)

                @block.scalar
                def _(act):
                    def gelu(g, j):
                        act.wait_ge(m["h_done"], at(g * FC + j + 1))
                        if j >= 2 or known(g, 1):
                            act.wait_ge(m["gl_done"], at(g * FC + j - 1))
                        nc.scalar.activation(g_t[:, j % 2], ps_h[j % 2][:], ACT.Gelu_apprx_tanh,
                                             bias=bias_cols[:, j:j + 1]).then_inc(m["gelu_done"], 1)

                    def flip(g, b):
                        act.wait_ge(m["m_xT_done"], at(g * MB + b + 1))
                        if known(g, 1):
                            act.wait_ge(m["h_done"], at(g * FC))
                        nc.scalar.copy(xT[:, HI, :, b * P:(b + 1) * P], ps_x[b % 2][:]).then_inc(m["m_xTh_done"], 1)

                    def high(g, j):
                        act.wait_ge(m["gelu_done"], at(g * FC + j + 1))
                        if j >= 2:
                            act.wait_ge(m["down_done"], at(g * (FC + MB - 1) + j - 1))
                        elif known(g, 1):
                            act.wait_ge(m["down_done"], at(g * (FC + MB - 1) - (MB if j == 0 else 0)))
                        nc.scalar.copy(g_r[:, j % 2, HI], g_t[:, j % 2]).then_inc(m["gh_done"], 1)

                    def steps(g, cur, prev, nxt):
                        if cur:
                            for j in range(FC):
                                gelu(g, j)
                                high(g, j)
                        if nxt:
                            for b in range(MB):
                                flip(g + 1, b)

                    run(act, steps)

                @block.vector
                def _(dve):
                    def low(g, j, stats=None):
                        if stats is not None:
                            dve.wait_ge(m["m_stats_done"], at(stats))
                        dve.wait_ge(m["gh_done"], at(g * FC + j + 1))
                        nc.vector.tensor_tensor(g_r[:, j % 2, LO], g_t[:, j % 2], g_r[:, j % 2, HI],
                                                ALU.subtract).then_inc(m["gl_done"], 1)

                    def flip(g, b):
                        dve.wait_ge(m["m_xTh_done"], at(g * MB + b + 1))
                        cols = slice(b * P, (b + 1) * P)
                        nc.vector.tensor_tensor(xT[:, LO, :, cols], ps_x[b % 2][:], xT[:, HI, :, cols],
                                                ALU.subtract).then_inc(m["m_xTl_done"], 1)

                    def statistics(g, b):
                        dve.wait_ge(m_x_in[b], at(16 * (g + 1)))
                        nc.vector.bn_stats(stat[:, b], x_t[:, b % 2]).then_inc(m["m_stats_done"], 1)

                    def norm(g, b):
                        k = g * MB + b + 1
                        nc.vector.bn_aggr(mv[:, b], stat[:, b]).then_inc(m["m_aggr_done"], 1)
                        dve.wait_ge(m["m_rstd_done"], at(k))
                        if known(g, 1):
                            dve.wait_ge(m["m_xT_done"], at(k - MB))
                        nc.vector.tensor_scalar(xn[:, b], x_t[:, b % 2], mv[:, b, 0:1], rstd[:, b], ALU.subtract,
                                                ALU.mult).then_inc(m["m_xn_done"], 1)

                    def output_row(g, b):
                        dve.wait_ge(m["down_done"], at(g * (FC + MB - 1) + FC + b))
                        dve.wait_ge(m["m_res_ready"], at(g * MB + b + 1))
                        nc.vector.tensor_tensor(res_t[:, b], ps_y[b][:], res_t[:, b],
                                                ALU.add).then_inc(m["m_y_done"], 1)

                    def steps(g, cur, prev, nxt):
                        if not cur:
                            for b in range(MB):
                                statistics(g + 1, b)
                                dve.wait_ge(m["m_stats_done"], (g + 1) * MB + b + 1)
                                norm(g + 1, b)
                        if cur:
                            for j in range(FC):
                                b = j - 4
                                normed = nxt and 0 <= b < MB
                                if normed:
                                    statistics(g + 1, b)
                                low(g, j, (g + 1) * MB + b + 1 if normed else None)
                                if normed:
                                    norm(g + 1, b)
                        if nxt:
                            for b in range(MB):
                                flip(g + 1, b)
                        if cur:
                            for b in range(MB):
                                output_row(g, b)

                    run(dve, steps)

                @block.gpsimd
                def _(pool):
                    def root(g, b):
                        pool.wait_ge(m["m_aggr_done"], at(g * MB + b + 1))
                        nc.gpsimd.tensor_tensor(rstd[:, b], mv[:, b, 1:2], eps_t[:], ALU.add
                                                ).then_inc(m["m_eps_added"], 1)
                        pool.wait_ge(m["m_eps_added"], at(g * MB + b + 1))
                        nc.gpsimd.tensor_tensor(rstd[:, b], rstd[:, b], neg_half[:], ALU.pow
                                                ).then_inc(m["m_rstd_done"], 1)

                    def steps(g, cur, prev, nxt):
                        if cur:
                            for b in range(MB):
                                pool.wait_ge(m_res_in[b], at(16 * (g + 1)))
                                nc.gpsimd.tensor_tensor(res_t[:, b], res_t[:, b], bias_row[:],
                                                        ALU.add).then_inc(m["m_res_ready"], 1)
                        if nxt:
                            for b in range(MB):
                                root(g + 1, b)

                    run(pool, steps)

        with ExitStack() as st:
            units = [(a["w_qkv"][:, H * i:H * (i + 1)], True) for i in range(3)] + [(a["w_ao"], False)]
            w = load_weights(st, st, units, a["ln1_s"], a["ln1_b"], [(a["b_qkv"], 0)], a["b_ao"], 3, 2 * KC)
            attention(st, w, 0, False, a["x"], None, a["mask_self"], x1_dram)
        with ExitStack() as st:
            units = ([(a["w_q"], True)] + [(a["w_kv"][:, H * i:H * (i + 1)], False) for i in range(2)]
                     + [(a["w_co"], False)])
            w = load_weights(st, st, units, a["ln2_s"], a["ln2_b"], [(a["b_q"], 0), (a["b_kv"], KC)], a["b_co"],
                             3, 2 * KC)
            attention(st, w, NG, True, x1_dram, a["ctx"], a["mask_cross"], x2_dram)
        with ExitStack() as st:
            units = ([(a["w1"][:, H * i:H * (i + 1)], True) for i in range(F // H)]
                     + [(a["w2"][H * i:H * (i + 1), :], False) for i in range(F // H)])
            w = load_weights(st, st, units, a["ln3_s"], a["ln3_b"], [(a["b1"], 0)], a["b2"])
            mlp(st, w, x2_dram, out)


_NAMES = {
    "x": "x", "ctx": "ctx_2048", "mask_self": "mask_1x1xSxS2_fc1", "mask_cross": "mask_Bx1xSxS2_ff1",
    **{n: f"L0_xattn_{n}" for n in ("ln1_s", "ln1_b", "w_qkv", "b_qkv", "w_ao", "b_ao", "ln2_s", "ln2_b", "w_q",
                                    "b_q", "w_kv", "b_kv", "w_co", "b_co", "ln3_s", "ln3_b", "w1", "b1", "w2",
                                    "b2")},
}


def kernel(**inputs):
    import numpy as _np
    import concourse.bacc as _bacc
    from concourse.bass_utils import run_bass_kernel_spmd as _run

    nc = _bacc.Bacc("TRN2", target_bir_lowering=False, num_devices=1)
    arrays, args = {}, {}
    for short, name in _NAMES.items():
        v = _np.ascontiguousarray(inputs[name])
        arrays[f"in_{short}"] = v
        args[short] = nc.dram_tensor(f"in_{short}", v.shape, mybir.dt.from_np(v.dtype), kind="ExternalInput").ap()
    shape = arrays["in_x"].shape
    out = nc.dram_tensor("out", shape, F32, kind="ExternalOutput").ap()
    xattn_layer(nc, args, out)
    r = _run(nc, [arrays], core_ids=[0])
    return r.results[0]["out"]
```

```python
import math
from contextlib import ExitStack

import concourse.bass as bass
from concourse import mybir
from concourse.alu_op_type import AluOpType as ALU

ACT = mybir.ActivationFunctionType
F32 = mybir.dt.float32
F32R = mybir.dt.float32r
F16 = mybir.dt.float16
BF16 = mybir.dt.bfloat16
AX_X = mybir.AxisListType.X

P = 128
NH = 16
HD = 32
HQ = P // HD
EPS = 1e-5
MASKED = 10000.0
LIFT = 15.0 * math.log(2.0)
VW = 3 * HD + 1
VPAD = VW + 1
HI, LO = 0, 1
PASSES = ((LO, HI), (HI, LO), (HI, HI))


class Looped:

    def __init__(self, register, rate, offset):
        self.register, self.rate, self.offset = register, rate, offset

    def __add__(self, k):
        return Looped(self.register, self.rate, self.offset + k)

    def __sub__(self, k):
        return self + -k

    def __mul__(self, k):
        return Looped(self.register, self.rate * k, self.offset * k)

    __rmul__ = __mul__


def at(x):
    if isinstance(x, Looped):
        assert x.offset >= 0
        return x.register * x.rate + x.offset
    assert x > 0 or isinstance(x, int)
    return x


def xattn_layer(nc, a, out):
    B, S, H = a["x"].shape
    KC = H // P
    F = a["w1"].shape[1]
    FC = F // P
    GB = 2
    NG = B // GB
    NS = KC * GB
    MB = 4
    NM = B // MB
    SCALE = 1.0 / math.sqrt(HD)
    assert S == P and NH * HD == H and KC == 4 and NG >= 4 and NM >= 2

    with ExitStack() as top:
        def sem(name):
            return top.enter_context(nc.semaphore(name))

        def sb(name, shape, dt=F32, where=top):
            return where.enter_context(nc.sbuf_tensor(name, shape, dt))

        def ps(name, shape, dt=F32, where=top):
            return where.enter_context(nc.psum_tensor(name, shape, dt))

        x1_dram = nc.dram_tensor("x_after_self", (B, S, H), F32, kind="Internal").ap()
        x2_dram = nc.dram_tensor("x_after_cross", (B, S, H), F32, kind="Internal").ap()

        ident = sb("ident", [P, P])
        ones = sb("ones", [P, 1])
        scale_t = sb("scale_t", [P, 1])
        eps_t = sb("eps_t", [P, 1])
        neg_half = sb("neg_half", [P, 1])
        lift_t = sb("lift_t", [P, 1])
        s_const = sem("const_ready")
        CONSTANTS = 7

        SELF, CROSS, UP, DOWN = range(4)
        WK, WQ, WV, WO = range(4)
        units = (
            [a["w_qkv"][:, H * i:H * (i + 1)] for i in (1, 0, 2)] + [a["w_ao"]],
            [a["w_kv"][:, 0:H], a["w_q"], a["w_kv"][:, H:2 * H], a["w_co"]],
            [a["w1"][:, H * i:H * (i + 1)] for i in range(F // H)],
            [a["w2"][H * i:H * (i + 1), :] for i in range(F // H)],
        )
        U = len(units[0])
        split_order = ((WK, WQ, WV, WO), (WV, WK, WQ, WO), range(U), range(U))
        assert all(len(u) == U for u in units)
        raw_wt, wt = [], []
        for i in range(3):
            with nc.sbuf_tensor(f"raw_wt{i}", [P, U, KC, H], F32) as place:
                raw_wt.append(place)
            wt.append(sb(f"wt{i}", [P, U, KC, H], F32R))
        LOW_AT = (1, 2, 1, 2)
        bias_cols = sb("bias_cols", [P, 3, U * KC])
        bias_row = sb("bias_row", [P, 3, H])
        norm_row = sb("norm_row", [P, 2, H])
        col_biases = (
            [(a["b_qkv"][H * i:H * (i + 1)], KC * u) for i, u in ((1, WK), (0, WQ), (2, WV))],
            [(a["b_kv"][0:H], KC * WK), (a["b_q"], KC * WQ), (a["b_kv"][H:2 * H], KC * WV)],
            [(a["b1"], 0)],
        )
        row_biases = (a["b_ao"], a["b_co"], a["b2"])
        norms = ((a["ln1_s"], a["ln1_b"]), (a["ln2_s"], a["ln2_b"]), (a["ln3_s"], a["ln3_b"]))

        raw_in = [[sem(f"raw_in{i}_{u}") for u in range(U)] for i in range(2)]
        par_in = [sem(f"par_in{st}") for st in range(3)]
        norm_in = sem("norm_in")
        w_hi_done, w_lo_done, w_lo_pool = sem("w_hi_done"), sem("w_lo_done"), sem("w_lo_pool_done")
        cv_ready, row_done, row_ready = sem("cv_ready"), sem("row_done"), sem("row_ready")

        def unit_no(st, u):
            return U * st + split_order[st].index(u) + 1

        def raw(st, u, c):
            return raw_wt[LOW_AT[st]][:, u, c]

        def arrived(st):
            return 16 * KC * (st // 2 + 1)

        def load_raw(sp, st, u, c):
            sp.dma_start(raw(st, u, c), units[st][u][c * P:(c + 1) * P, :]).then_inc(raw_in[st % 2][u], 16)

        def par_loads(st):
            return 16 * (1 + len(col_biases[st]))

        def load_params(sp, st):
            for vec, k in col_biases[st]:
                sp.dma_start(bias_cols[:, st, k:k + vec.shape[0] // P], vec.rearrange("(c p) -> p c", p=P),
                             allow_slow_non_contiguous=True).then_inc(par_in[st], 16)
            sp.dma_start(bias_row[:, st], row_biases[st].rearrange("(a n) -> a n", a=1).to_broadcast([P, H])
                         ).then_inc(par_in[st], 16)

        def load_norm(sp, st):
            for i, vec in enumerate(norms[st]):
                sp.dma_start(norm_row[:, i], vec.rearrange("(a n) -> a n", a=1).to_broadcast([P, H])
                             ).then_inc(norm_in, 16)

        def high_weights(act, st, u, hi_t):
            act.wait_ge(raw_in[st % 2][u], arrived(st))
            for c in range(KC):
                nc.scalar.copy(hi_t[:, u, c], raw(st, u, c)).then_inc(w_hi_done, 1)

        def low_weights(engine, st, u, hi_t, pieces, done):
            for c in pieces:
                engine.wait_ge(w_hi_done, KC * (unit_no(st, u) - 1) + c + 1)
                last = engine.tensor_tensor(wt[LOW_AT[st]][:, u, c], raw(st, u, c), hi_t[:, u, c], ALU.subtract)
            last.then_inc(done, 1)

        DVE_PIECES, POOL_PIECES = range(0, KC, 2), range(1, KC, 2)

        def wait_split(pe, st, u):
            pe.wait_ge(w_lo_done, unit_no(st, u))
            pe.wait_ge(w_lo_pool, unit_no(st, u))

        x_in = [sem(f"x_in{b}") for b in range(GB)]
        enc_in = [sem(f"enc_in{b}") for b in range(GB)]
        mask_in = [sem(f"mask_in{b}") for b in range(GB)]
        res_in = [sem(f"res_in{b}") for b in range(GB)]
        stored = [sem(f"stored{b}") for b in range(GB)]
        kbd_in = [sem(f"kbd_in{i}") for i in range(2)]
        names = ("sc_done pt_done pv_done k_done q_done v_done o_done xT_done encT_done cT_done exp_done pth_done "
                 "kh_done qh_done v1_done v2_done xTh_done encTh_done cTh_done masked mx_done nb_done ptl_done "
                 "kl_done ql_done vr_done v0_done y_copied xTl_done encTl_done cTl_done stats_done aggr_done rstd_done xn_done "
                 "centred eps_added sums_done ctx_done y_done biased v3_done mask_ready res_ready kbd_clear ones_ready")
        s = {name: sem(name) for name in names.split()}

        def attention(st):

            def buf(name, shape, dt=F32):
                return sb(f"a_{name}", shape, dt, st)

            x_t = buf("x_t", [P, GB, H])
            xn = buf("xn", [P, GB, H])
            enc_t = buf("enc_t", [P, GB, H])
            res_t = buf("res_t", [P, GB, H])
            y_t = buf("y_t", [P, GB, H])
            m_raw = buf("m_raw", [P, GB, P])
            m_mul = buf("m_mul", [P, GB, P])
            m_add = buf("m_add", [P, GB, P])
            xT = buf("xT", [P, 2, KC, GB * P], F32R)
            encT = buf("encT", [P, 2, KC, GB * P], F32R)
            q_r = buf("q_r", [P, 2, 2, GB * P], F32R)
            k_r = buf("k_r", [P, 2, 2, GB * P], F32R)
            k_bd = buf("k_bd", [P, 2, 2, GB, HQ * P], F32R)
            v_b = buf("v_b", [P, GB, NH, VPAD], BF16)
            v_rest = buf("v_rest", [P, GB, H])
            t_s = buf("t_s", [P, 2, HQ, P])
            p_s = buf("p_s", [P, 2, HQ, P])
            mx = buf("mx", [P, 2, HQ])
            nb = buf("nb", [P, 2, HQ])
            pT = buf("pT", [P, 2, 2, HQ * P], F16)
            csum = buf("csum", [P, 2, HQ, HD])
            rcp = buf("rcp", [P, 2, HQ])
            ctx_t = buf("ctx_t", [P, GB, H])
            cT = buf("cT", [P, GB, 2, KC, P], F32R)
            stat = buf("stat", [P, GB, 6])
            mv = buf("mv", [P, GB, 2])
            rstd = buf("rstd", [P, GB, 1])
            cv = buf("cv", [P, KC, P])

            ps_s = [ps(f"a_ps_s{i}", [P, HQ, P], F32, st) for i in range(2)]
            ps_t = [ps(f"a_ps_t{i}", [P, HQ, P], F32, st) for i in range(2)]
            ps_c = ps(f"a_ps_c", [P, H], F32, st)
            ps_r = ps(f"a_ps_r", [P, H], F32, st)
            ps_o = ps(f"a_ps_o", [P, HQ, P], F32, st)
            ps_x = ps(f"a_ps_x", [P, KC, P], F32, st)

            gN = 2 * NG

            def crosses(g):
                return (g.offset if isinstance(g, Looped) else g) >= NG

            def opens(g):
                return isinstance(g, int) and g in (0, NG)

            def weights(g, h):
                return wt[0 if h == HI else LOW_AT[crosses(g)]]

            def lag(g, n, by):
                return (g, n - by) if n >= by else (g - 1, n - by + NS)

            def slot_no(g, n):
                return g * NS + n + 1

            def run(engine, slot):
                for n in range(4, NS):
                    slot(-1, n, False, False, True)
                for n in range(NS):
                    slot(0, n, True, False, True)
                for n in range(NS):
                    slot(1, n, True, True, True)
                with engine.Fori(0, NG - 3) as i:
                    g = Looped(i, 1, 2)
                    for n in range(NS):
                        slot(g, n, True, True, True)
                for g in (NG - 1, NG, NG + 1):
                    for n in range(NS):
                        slot(g, n, True, True, True)
                with engine.Fori(0, NG - 3) as i:
                    g = Looped(i, 1, NG + 2)
                    for n in range(NS):
                        slot(g, n, True, True, True)
                for n in range(NS):
                    slot(gN - 1, n, True, True, False)
                for n in range(NS):
                    slot(gN, n, False, True, False)

            def units_split(g, n):
                if isinstance(g, int):
                    if g == -1 and n < 7:
                        return [(SELF, n - 4)]
                    if g == NG - 1 and n in (3, 4, 5):
                        return [(CROSS, (WV, WK, WQ)[n - 3])]
                    if opens(g - 1) and n == 0:
                        return [(int(crosses(g - 1)), WO)]
                    if g == gN and n in (0, 1, 2, 7):
                        return [(UP, min(n, WO))]
                return []

            def known(g, least):
                return not isinstance(g, int) or g >= least

            with nc.Block() as block:
                @block.sync
                def _(sp):
                    def row(g, b):
                        r = (g - NG if crosses(g) else g) * GB + b
                        return r if isinstance(r, int) else bass.ds(at(r), 1)

                    def load_x(g, b):
                        if known(g, 1):
                            sp.wait_ge(s["xn_done"], at(g * GB - GB + b + 1))
                        src = x1_dram if crosses(g) else a["x"]
                        sp.dma_start(x_t[:, b], src[row(g, b)]).then_inc(x_in[b], 16)

                    def load_enc(g, b):
                        if known(g, NG + 1):
                            sp.wait_ge(s["encT_done"], at((g - NG) * GB - GB + b + 1))
                        sp.dma_start(enc_t[:, b], a["ctx"][row(g, b)]).then_inc(enc_in[b], 16)

                    def load_mask(g, b):
                        if known(g, 1):
                            sp.wait_ge(s["mask_ready"], at(2 * ((g - 1) * GB + b + 1)))
                        src = a["mask_cross"][row(g, b), 0] if crosses(g) else a["mask_self"][0, 0]
                        sp.dma_start(m_raw[:, b], src).then_inc(mask_in[b], 16)

                    def load_res(g, b):
                        if known(g, 1):
                            sp.wait_ge(s["y_done"], at((g - 1) * GB + b + 1))
                        src = x1_dram if crosses(g) else a["x"]
                        sp.dma_start(res_t[:, b], src[row(g, b)]).then_inc(res_in[b], 16)

                    def place_k(g, c):
                        i = c % 2
                        sp.wait_ge(s["kl_done"], at(g * KC + c + 1))
                        if c < 2 and not known(g, 1):
                            sp.wait_ge(s["kbd_clear"], 1)
                        for j in range(HQ):
                            r = slice(HD * j, HD * (j + 1))
                            sp.dma_start(
                                k_bd[r, i, :, :, P * j:P * (j + 1)].rearrange("p h b t -> p (h b) t").bitcast(F32),
                                k_r[r, i].rearrange("p h (b t) -> p (h b) t", b=GB).bitcast(F32)
                                ).then_inc(kbd_in[i], 16)

                    def store(g, b):
                        sp.wait_ge(s["y_done"], at(g * GB + b + 1))
                        dst = x2_dram if crosses(g) else x1_dram
                        sp.dma_start(dst[row(g, b)], y_t[:, b]).then_inc(stored[b], 16)

                    def weight_piece(g, n):
                        if not isinstance(g, int):
                            return
                        if g in (0, 1):
                            if g == 0 and n == 0:
                                load_params(sp, CROSS)
                            load_raw(sp, CROSS, *divmod(g * NS + n, KC))
                        if g == NG - 1 and n == 0:
                            sp.wait_ge(s["xn_done"], NG * GB)
                            load_norm(sp, CROSS)
                        if g in (NG + 1, gN - 1):
                            if g == NG + 1 and n == 0:
                                sp.wait_ge(s["o_done"], NG * GB)
                                load_params(sp, UP)
                            load_raw(sp, UP, *divmod((g == gN - 1) * NS + n, KC))
                        if g == gN and n == 0:
                            sp.wait_ge(s["xn_done"], gN * GB)
                            load_norm(sp, UP)
                        if g == gN and n < 3:
                            done, count = (("k_done", KC), ("q_done", KC), ("v_done", GB))[n]
                            sp.wait_ge(s[done], gN * count)
                            for c in range(KC):
                                load_raw(sp, DOWN, n, c)

                    def slot(g, n, cur, prev, nxt):
                        if n == 0 and isinstance(g, int) and g in (NG - 1, NG + 1):
                            for b in range(GB):
                                sp.wait_ge(stored[b], 16 * (NG - 2 if g == NG - 1 else NG))
                        if n == 0 and cur and nxt:
                            load_x(g + 1, 0)
                            load_x(g + 1, 1)
                        if n in (1, 3) and cur:
                            place_k(g, (n + 3) // 2)
                        if n == 1 and cur and nxt and crosses(g + 1):
                            load_enc(g + 1, 0)
                            load_enc(g + 1, 1)
                        if n == 3 and cur and nxt:
                            load_mask(g + 1, 0)
                            load_mask(g + 1, 1)
                        if n in (5, 7) and prev:
                            store(g - 1, (n - 5) // 2)
                        if n in (5, 7) and nxt:
                            place_k(g + 1, (n - 5) // 2)
                        if n in (1, 2) and prev:
                            load_res(g - 1, n - 1)
                        weight_piece(g, n)

                    for b in range(GB):
                        load_x(0, b)
                    load_norm(sp, SELF)
                    for c in range(KC):
                        load_raw(sp, SELF, WK, c)
                    load_params(sp, SELF)
                    for u in (WQ, WV):
                        for c in range(KC):
                            load_raw(sp, SELF, u, c)
                    for b in range(GB):
                        load_mask(0, b)
                    for c in range(KC):
                        load_raw(sp, SELF, WO, c)
                    run(sp, slot)
                    for b in range(GB):
                        sp.wait_ge(stored[b], 16 * gN)

                @block.tensor
                def _(pe):
                    def scores(g, n):
                        c, b = divmod(n, GB)
                        i = c % 2
                        pe.wait_ge(kbd_in[i], at(g * (16 * HQ * KC // 2) + 16 * HQ * (c // 2 + 1)))
                        pe.wait_ge(s["ql_done"], at(g * KC + c + 1))
                        if n >= 2 or known(g, 1):
                            pe.wait_ge(s["masked"], at(slot_no(*lag(g, n, 2))))
                        for x, (hq, hk) in enumerate(PASSES):
                            last = nc.tensor.matmul(ps_s[n % 2][:], q_r[:, i, hq, b * P:(b + 1) * P],
                                                    k_bd[:, i, hk, b], start=(x == 0), stop=(x == 2))
                        last.then_inc(s["sc_done"], 1)

                    def transpose_probs(g, n):
                        pe.wait_ge(s["exp_done"], at(slot_no(g, n)))
                        if n >= 2 or known(g, 1):
                            pe.wait_ge(s["ptl_done"], at(slot_no(*lag(g, n, 2))))
                        for j in range(HQ):
                            last = nc.tensor.transpose(ps_t[n % 2][:, j], p_s[:, n % 2, j], ident[:])
                        last.then_inc(s["pt_done"], 1)

                    def weigh_values(g, n):
                        c, b = divmod(n, GB)
                        pe.wait_ge(s["ptl_done"], at(slot_no(g, n)))
                        if c == 0:
                            pe.wait_ge(s["v3_done"], at(g * GB + b + 1))
                        if n >= 1 or known(g, 1):
                            pe.wait_ge(s["sums_done"], at(2 * slot_no(*lag(g, n, 1))))
                        for j in range(HQ):
                            for h in (HI, LO):
                                last = nc.tensor.matmul(ps_o[:, j, 0:VW], pT[:, n % 2, h, j * P:(j + 1) * P],
                                                        v_b[:, b, HQ * c + j, 0:VW], start=(h == HI), stop=(h == LO))
                        last.then_inc(s["pv_done"], 1)

                    def columns(g, unit, xt, c, done):
                        k = 0
                        for hw, hx in PASSES:
                            for kc in range(KC):
                                last = nc.tensor.matmul(ps_c[:, 0:GB * P],
                                                        weights(g, hw)[:, unit, kc, c * P:(c + 1) * P],
                                                        xt[:, hx, kc], start=(k == 0), stop=(k == 3 * KC - 1))
                                k += 1
                        last.then_inc(s[done], 1)

                    def rows(g, unit, half, lhs, done):
                        steps = [(hx, hw, kc) for hx, hw in PASSES for kc in range(KC)]
                        n = len(steps) // 2
                        for k in range(half * n, half * n + n):
                            hx, hw, kc = steps[k]
                            last = nc.tensor.matmul(ps_r[:], lhs(hx, kc), weights(g, hw)[:, unit, kc],
                                                    start=(k == 0), stop=(k == 2 * n - 1))
                        if half == 1:
                            last.then_inc(s[done], 1)

                    def keys(g, c):
                        if c == 0:
                            if crosses(g):
                                pe.wait_ge(s["encTl_done"], at((g - NG + 1) * GB))
                            else:
                                pe.wait_ge(s["xTl_done"], at((g + 1) * GB))
                            if opens(g):
                                wait_split(pe, crosses(g), WK)
                        if c > 0 or known(g, 1):
                            pe.wait_ge(s["ql_done"], at(g * KC + c))
                        columns(g, WK, encT if crosses(g) else xT, c, "k_done")

                    def queries(g, c):
                        if c == 0:
                            pe.wait_ge(s["xTl_done"], at((g + 1) * GB))
                            if opens(g):
                                wait_split(pe, crosses(g), WQ)
                        pe.wait_ge(s["kl_done"], at(g * KC + c + 1))
                        columns(g, WQ, xT, c, "q_done")

                    def values(g, b, half):
                        if half == 0:
                            if b == 1:
                                pe.wait_ge(s["v1_done"], at(g * GB + 1))
                            elif known(g, 2):
                                pe.wait_ge(s["y_copied"], at((g - 1) * GB))
                            elif known(g, 1):
                                pe.wait_ge(s["v1_done"], at(g * GB))
                            if b == 0 and opens(g):
                                wait_split(pe, crosses(g), WV)
                        kv_t = encT if crosses(g) else xT
                        rows(g, WV, half, lambda h, kc: kv_t[:, h, kc, b * P:(b + 1) * P], "v_done")

                    def outputs(g, b, half, cur):
                        if half == 0:
                            pe.wait_ge(s["cTl_done"], at(g * GB + b + 1))
                            if b == 1:
                                pe.wait_ge(s["y_copied"], at(g * GB + 1))
                            elif cur:
                                pe.wait_ge(s["v1_done"], at((g + 2) * GB))
                            else:
                                pe.wait_ge(s["y_copied"], at(g * GB))
                            if b == 0 and opens(g):
                                wait_split(pe, crosses(g), WO)
                        rows(g, WO, half, lambda h, kc: cT[:, b, h, kc], "o_done")

                    def flip(src, b, done):
                        for kc in range(KC):
                            last = nc.tensor.transpose(ps_x[:, kc], src[:, b, kc * P:(kc + 1) * P], ident[:])
                        last.then_inc(s[done], 1)

                    def flip_ctx(g, b):
                        pe.wait_ge(s["ctx_done"], at(slot_no(g, NS - GB + b)))
                        if b == 0:
                            if known(g, gN - 1):
                                pe.wait_ge(s["xTl_done"], at((g + 1) * GB))
                            else:
                                pe.wait_ge(s["xTl_done"], at((g + 2) * GB))
                            if opens(g):
                                pe.wait_ge(row_ready, 1 + crosses(g))
                        else:
                            pe.wait_ge(s["cTl_done"], at(g * GB + b))
                        flip(ctx_t, b, "cT_done")

                    def flip_x(g, b):
                        pe.wait_ge(s["xn_done"], at(g * GB + b + 1))
                        if b == 1:
                            pe.wait_ge(s["xTl_done"], at(g * GB + b))
                        elif crosses(g):
                            pe.wait_ge(s["encTl_done"], at((g - NG) * GB + 2))
                        elif known(g, 2):
                            pe.wait_ge(s["cTl_done"], at((g - 1) * GB))
                        elif known(g, 1):
                            pe.wait_ge(s["xTl_done"], at(g * GB))
                        flip(xn, b, "xT_done")

                    def flip_enc(g, b):
                        pe.wait_ge(enc_in[b], at(16 * (g - NG + 1)))
                        if b == 1:
                            pe.wait_ge(s["encTl_done"], at((g - NG) * GB + b))
                        else:
                            pe.wait_ge(s["cTl_done"], at((g - 1) * GB))
                        flip(enc_t, b, "encT_done")

                    def slot(g, n, cur, prev, nxt):
                        if cur:
                            scores(g, n)
                        if cur if n >= 2 else prev:
                            transpose_probs(*lag(g, n, 2))
                        if cur if n >= 3 else prev:
                            weigh_values(*lag(g, n, 3))
                        if n in (2, 3) and prev:
                            flip_ctx(g - 1, n - 2)
                        if n == 5 and nxt:
                            (flip_enc if crosses(g + 1) else flip_x)(g + 1, 1)
                        if n == 6 and nxt and crosses(g + 1):
                            flip_x(g + 1, 1)
                        if n in (0, 2, 4) and cur:
                            queries(g, (n + 2) // 2)
                        if n in (1, 3) and cur:
                            keys(g, (n + 3) // 2)
                        if n == 7 and nxt:
                            keys(g + 1, 1)
                        if n in (3, 4, 5, 6) and prev:
                            outputs(g - 1, (n - 3) // 2, (n - 3) % 2, cur)
                        if n == 7 and nxt:
                            values(g + 1, 0, 0)
                        if n in (0, 1, 2) and cur:
                            values(g, (n + 1) // 2, (n + 1) % 2)
                        if n == 4 and nxt:
                            (flip_enc if crosses(g + 1) else flip_x)(g + 1, 0)
                        if n == 5 and nxt:
                            if crosses(g + 1):
                                flip_x(g + 1, 0)
                            keys(g + 1, 0)
                        if n == 6 and nxt:
                            queries(g + 1, 0)
                        if n == 7 and opens(g):
                            bias_products(g)

                    def bias_products(g):
                        st = int(crosses(g))
                        pe.wait_ge(s["xTl_done"], (g + 2) * GB)
                        pe.wait_ge(raw_in[st % 2][WO], arrived(st))
                        pe.wait_ge(cv_ready, st + 1)
                        for c in range(KC):
                            last = nc.tensor.matmul(ps_x[:].rearrange("p c t -> p (c t)"), cv[:, c],
                                                    raw(st, WO, c), start=(c == 0), stop=(c == KC - 1))
                        last.then_inc(row_done, 1)

                    pe.wait_ge(s_const, CONSTANTS)
                    run(pe, slot)

                @block.scalar
                def _(act):
                    def high_probs(g, n):
                        act.wait_ge(s["pt_done"], at(slot_no(g, n)))
                        if n >= 2 or known(g, 1):
                            act.wait_ge(s["pv_done"], at(slot_no(*lag(g, n, 2))))
                        nc.scalar.copy(pT[:, n % 2, HI], ps_t[n % 2][:].rearrange("p j t -> p (j t)")
                                       ).then_inc(s["pth_done"], 1)

                    def exponent(g, n):
                        act.wait_ge(s["mx_done"], at(slot_no(g, n)))
                        if n >= 2 or known(g, 1):
                            act.wait_ge(s["exp_done"], at(slot_no(*lag(g, n, 2))))
                        nc.scalar.activation(nb[:, n % 2], mx[:, n % 2], ACT.Identity, bias=lift_t[:],
                                             scale=-1.0).then_inc(s["nb_done"], 1)
                        act.wait_ge(s["nb_done"], at(slot_no(g, n)))
                        if n >= 2 or known(g, 1):
                            act.wait_ge(s["pt_done"], at(slot_no(*lag(g, n, 2))))
                        for j in range(HQ):
                            last = nc.scalar.activation(p_s[:, n % 2, j], t_s[:, n % 2, j], ACT.Exp,
                                                        bias=nb[:, n % 2, j:j + 1])
                        last.then_inc(s["exp_done"], 1)

                    def high_cols(g, c, unit, dst_t, done, high):
                        act.wait_ge(s[done], at(g * KC + c + 1))
                        i = c % 2
                        if c >= 2:
                            act.wait_ge(s["sc_done"], at(slot_no(g, (c - 1) * GB - 1)))
                        elif known(g, 1):
                            act.wait_ge(s["sc_done"], at(slot_no(g - 1, (c + KC - 1) * GB - 1)))
                        if unit == WK:
                            if c >= 2 or known(g, 1):
                                act.wait_ge(kbd_in[i], at(g * (16 * HQ * KC // 2) + 16 * HQ * (c // 2)))
                        if c == 0 and opens(g):
                            act.wait_ge(par_in[crosses(g)], par_loads(crosses(g)))
                        nc.scalar.activation(dst_t[:, i, HI], ps_c[:, 0:GB * P], ACT.Identity,
                                             bias=bias_cols[:, crosses(g), KC * unit + c:KC * unit + c + 1]
                                             ).then_inc(s[high], 1)

                    def value_top(g, b):
                        act.wait_ge(s["v_done"], at(g * GB + b + 1))
                        if known(g, 1):
                            act.wait_ge(s["v3_done"], at(g * GB + b - 1))
                        nc.scalar.copy(v_rest[:, b], ps_r[:]).then_inc(s["v0_done"], 1)
                        if known(g, 1):
                            act.wait_ge(s["pv_done"], at(slot_no(g - 1, NS - GB + b)))
                        else:
                            act.wait_ge(s["ones_ready"], 1)
                        nc.scalar.copy(v_b[:, b, :, 0:HD], ps_r[:].rearrange("p (h d) -> p h d", h=NH)
                                       ).then_inc(s["v1_done"], 1)

                    def value_middle(g, b):
                        act.wait_ge(s["vr_done"], at(g * GB + b + 1))
                        nc.scalar.copy(v_b[:, b, :, HD:2 * HD], v_rest[:, b].rearrange("p (h d) -> p h d", h=NH)
                                       ).then_inc(s["v2_done"], 1)

                    def output_row(g, b):
                        act.wait_ge(s["o_done"], at(g * GB + b + 1))
                        if known(g, 1):
                            act.wait_ge(stored[b], at(16 * g))
                        nc.scalar.copy(y_t[:, b], ps_r[:]).then_inc(s["y_copied"], 1)

                    def high_flip(dst_t, done, count, free, high):
                        act.wait_ge(s[done], at(count))
                        for name, value in free:
                            act.wait_ge(s[name], at(value))
                        nc.scalar.copy(dst_t, ps_x[:]).then_inc(s[high], 1)

                    def flip_x(g, b):
                        free = [("q_done", g * KC)] if known(g, 1) else []
                        high_flip(xT[:, HI, :, b * P:(b + 1) * P], "xT_done", g * GB + b + 1, free, "xTh_done")

                    def flip_enc(g, b):
                        free = [("k_done", g * KC)] if known(g, NG + 1) else []
                        high_flip(encT[:, HI, :, b * P:(b + 1) * P], "encT_done", (g - NG) * GB + b + 1, free,
                                  "encTh_done")

                    def flip_ctx(g, b):
                        free = [("o_done", (g - 1) * GB + b + 1)] if known(g, 1) else []
                        high_flip(cT[:, b, HI], "cT_done", g * GB + b + 1, free, "cTh_done")

                    def slot(g, n, cur, prev, nxt):
                        if n in (1, 3) and cur:
                            value_top(g, n // 2)
                        if n in (5, 7) and prev:
                            output_row(g - 1, (n - 5) // 2)
                        if cur if n >= 2 else prev:
                            high_probs(*lag(g, n, 2))
                        if n in (2, 3) and prev:
                            flip_ctx(g - 1, n - 2)
                        if n == 5 and nxt:
                            (flip_enc if crosses(g + 1) else flip_x)(g + 1, 1)
                        if n == 6 and nxt and crosses(g + 1):
                            flip_x(g + 1, 1)
                        if cur if n >= 1 else prev:
                            exponent(*lag(g, n, 1))
                        split_weights(g, n)
                        if n in (0, 2, 4) and cur:
                            high_cols(g, n // 2 + 1, WQ, q_r, "q_done", "qh_done")
                        if n in (1, 3) and cur:
                            high_cols(g, (n + 3) // 2, WK, k_r, "k_done", "kh_done")
                        if n == 7 and nxt:
                            high_cols(g + 1, 1, WK, k_r, "k_done", "kh_done")
                        if n in (1, 3) and cur:
                            value_middle(g, n // 2)
                        if n == 4 and nxt:
                            (flip_enc if crosses(g + 1) else flip_x)(g + 1, 0)
                        if n == 5 and nxt:
                            if crosses(g + 1):
                                flip_x(g + 1, 0)
                            high_cols(g + 1, 0, WK, k_r, "k_done", "kh_done")
                        if n == 6 and nxt:
                            high_cols(g + 1, 0, WQ, q_r, "q_done", "qh_done")

                    def split_weights(g, n):
                        if not isinstance(g, int):
                            return
                        if g == -1 and n < 7:
                            high_weights(act, SELF, n - 4, wt[0])
                        if g == NG - 1 and n in (3, 4, 5):
                            u, done, count = ((WV, "v_done", GB), (WK, "k_done", KC), (WQ, "q_done", KC))[n - 3]
                            act.wait_ge(s[done], NG * count)
                            high_weights(act, CROSS, u, wt[0])
                        if opens(g - 1) and n == 0:
                            if crosses(g - 1):
                                act.wait_ge(s["o_done"], NG * GB)
                            high_weights(act, crosses(g - 1), WO, wt[0])
                        if g == gN and n in (0, 1, 2, 7):
                            u = min(n, WO)
                            done, count = (("k_done", KC), ("q_done", KC), ("v_done", GB), ("o_done", GB))[u]
                            act.wait_ge(s[done], gN * count)
                            high_weights(act, UP, u, wt[0])

                    act.wait_ge(s_const, CONSTANTS)
                    run(act, slot)

                @block.vector
                def _(dve):
                    def mask_scores(g, n):
                        b = n % GB
                        dve.wait_ge(s["sc_done"], at(slot_no(g, n)))
                        if n < GB:
                            dve.wait_ge(s["mask_ready"], at(2 * (g * GB + b + 1)))
                        if n >= 2 or known(g, 1):
                            dve.wait_ge(s["exp_done"], at(slot_no(*lag(g, n, 2))))
                        nc.vector.tensor_tensor(t_s[:, n % 2], ps_s[n % 2][:],
                                                m_mul[:, b].unsqueeze(1).to_broadcast([P, HQ, P]),
                                                ALU.mult).then_inc(s["masked"], 1)

                    def low_probs(g, n):
                        dve.wait_ge(s["pth_done"], at(slot_no(g, n)))
                        nc.vector.tensor_tensor(pT[:, n % 2, LO], ps_t[n % 2][:].rearrange("p j t -> p (j t)"),
                                                pT[:, n % 2, HI], ALU.subtract).then_inc(s["ptl_done"], 1)

                    def maxima(g, n):
                        dve.wait_ge(s["biased"], at(slot_no(g, n)))
                        if n >= 2 or known(g, 1):
                            dve.wait_ge(s["nb_done"], at(slot_no(*lag(g, n, 2))))
                        nc.vector.tensor_reduce(mx[:, n % 2], t_s[:, n % 2], AX_X, ALU.max).then_inc(s["mx_done"], 1)

                    def context(g, n, stats=None):
                        c, b = divmod(n, GB)
                        if stats is not None:
                            dve.wait_ge(s["stats_done"], at(stats))
                        dve.wait_ge(s["pv_done"], at(slot_no(g, n)))
                        if n >= 2 or known(g, 1):
                            dve.wait_ge(s["ctx_done"], at(slot_no(*lag(g, n, 2))))
                        nc.vector.tensor_reduce(csum[:, n % 2], ps_o[:, :, 0:3 * HD].rearrange(
                            "p j (t d) -> p j d t", t=3), AX_X, ALU.add).then_inc(s["sums_done"], 1)
                        nc.vector.reciprocal(rcp[:, n % 2], ps_o[:, :, 3 * HD]).then_inc(s["sums_done"], 1)
                        dve.wait_ge(s["sums_done"], at(2 * slot_no(g, n)))
                        if c == 0 and known(g, 1):
                            dve.wait_ge(s["cT_done"], at((g - 1) * GB + b + 1))
                        nc.vector.tensor_tensor(ctx_t[:, b, c * P:(c + 1) * P].rearrange("p (j d) -> p j d", j=HQ),
                                                csum[:, n % 2],
                                                rcp[:, n % 2].unsqueeze(2).to_broadcast([P, HQ, HD]),
                                                ALU.mult).then_inc(s["ctx_done"], 1)

                    def low_cols(g, c, unit, dst_t, high, low):
                        dve.wait_ge(s[high], at(g * KC + c + 1))
                        i = c % 2
                        nc.vector.scalar_tensor_tensor(
                            out=dst_t[:, i, LO], in0=ps_c[:, 0:GB * P],
                            scalar=bias_cols[:, crosses(g), KC * unit + c:KC * unit + c + 1], in1=dst_t[:, i, HI],
                            op0=ALU.add, op1=ALU.subtract).then_inc(s[low], 1)

                    def low_flip(hi_t, lo_t, high, count, low):
                        dve.wait_ge(s[high], at(count))
                        nc.vector.tensor_tensor(lo_t, ps_x[:], hi_t, ALU.subtract).then_inc(s[low], 1)

                    def flip_x(g, b):
                        cols = slice(b * P, (b + 1) * P)
                        low_flip(xT[:, HI, :, cols], xT[:, LO, :, cols], "xTh_done", g * GB + b + 1, "xTl_done")

                    def flip_enc(g, b):
                        cols = slice(b * P, (b + 1) * P)
                        low_flip(encT[:, HI, :, cols], encT[:, LO, :, cols], "encTh_done", (g - NG) * GB + b + 1,
                                 "encTl_done")

                    def flip_ctx(g, b):
                        low_flip(cT[:, b, HI], cT[:, b, LO], "cTh_done", g * GB + b + 1, "cTl_done")

                    def statistics(g, b):
                        dve.wait_ge(x_in[b], at(16 * (g + 1)))
                        nc.vector.bn_stats(stat[:, b], x_t[:, b]).then_inc(s["stats_done"], 1)

                    def moments(g, b):
                        nc.vector.bn_aggr(mv[:, b], stat[:, b]).then_inc(s["aggr_done"], 1)

                    def centre(g, b):
                        k = g * GB + b + 1
                        dve.wait_ge(s["aggr_done"], at(k))
                        if known(g, 1):
                            dve.wait_ge(s["xT_done"], at(k - GB))
                        if opens(g) and b == 0:
                            dve.wait_ge(norm_in, 32 * (1 + crosses(g)))
                        nc.vector.scalar_tensor_tensor(
                            out=xn[:, b], in0=x_t[:, b], scalar=mv[:, b, 0:1], in1=norm_row[:, 0],
                            op0=ALU.subtract, op1=ALU.mult).then_inc(s["centred"], 1)

                    def norm(g, b):
                        k = g * GB + b + 1
                        dve.wait_ge(s["centred"], at(k))
                        dve.wait_ge(s["rstd_done"], at(k))
                        nc.vector.scalar_tensor_tensor(
                            out=xn[:, b], in0=xn[:, b], scalar=rstd[:, b], in1=norm_row[:, 1],
                            op0=ALU.mult, op1=ALU.add).then_inc(s["xn_done"], 1)

                    def slot(g, n, cur, prev, nxt):
                        ahead = cur and nxt
                        if n == 4 and ahead:
                            norm(g + 1, 1)
                        if cur if n >= 1 else prev:
                            maxima(*lag(g, n, 1))
                        if cur:
                            mask_scores(g, n)
                        if cur if n >= 2 else prev:
                            low_probs(*lag(g, n, 2))
                        if n in (1, 2) and ahead:
                            statistics(g + 1, n - 1)
                        if n in (2, 3) and prev:
                            flip_ctx(g - 1, n - 2)
                        if n == 5 and nxt:
                            (flip_enc if crosses(g + 1) else flip_x)(g + 1, 1)
                        if n == 6 and nxt and crosses(g + 1):
                            flip_x(g + 1, 1)
                        if cur if n >= 3 else prev:
                            context(*lag(g, n, 3), (g + 1) * GB + n if n in (1, 2) and ahead else None)
                        if n in (1, 2) and ahead:
                            if not prev:
                                dve.wait_ge(s["stats_done"], (g + 1) * GB + n)
                            moments(g + 1, n - 1)
                        split_weights(g, n)
                        if n in (0, 2, 4) and cur:
                            low_cols(g, n // 2 + 1, WQ, q_r, "qh_done", "ql_done")
                        if n in (1, 3) and cur:
                            low_cols(g, (n + 3) // 2, WK, k_r, "kh_done", "kl_done")
                        if n == 7 and nxt:
                            low_cols(g + 1, 1, WK, k_r, "kh_done", "kl_done")
                        if n == 4 and nxt:
                            (flip_enc if crosses(g + 1) else flip_x)(g + 1, 0)
                        if n == 5 and nxt:
                            if crosses(g + 1):
                                flip_x(g + 1, 0)
                            low_cols(g + 1, 0, WK, k_r, "kh_done", "kl_done")
                        if n == 6 and nxt:
                            low_cols(g + 1, 0, WQ, q_r, "qh_done", "ql_done")
                        if n in (1, 3) and ahead:
                            centre(g + 1, n // 2)
                        if n == 3 and ahead:
                            norm(g + 1, 0)

                    def spread_value_bias(st):
                        dve.wait_ge(par_in[st], par_loads(st))
                        if st == CROSS:
                            dve.wait_ge(row_done, 1)
                        for c in range(KC):
                            k = KC * WV + c
                            last = nc.vector.tensor_scalar(cv[:, c], ones[:].to_broadcast([P, P]), bias_cols[:, st, k:k + 1], None,
                                                           ALU.mult)
                        last.then_inc(cv_ready, 1)

                    def add_row(st):
                        dve.wait_ge(row_done, st + 1)
                        nc.vector.tensor_tensor(bias_row[:, st], ps_x[:].rearrange("p c t -> p (c t)"),
                                                bias_row[:, st], ALU.add).then_inc(row_ready, 1)

                    def split_weights(g, n):
                        if not isinstance(g, int):
                            return
                        if opens(g) and n == 6:
                            spread_value_bias(int(crosses(g)))
                        if opens(g - 1) and n == 0:
                            add_row(int(crosses(g - 1)))
                        for st, u in units_split(g, n):
                            low_weights(nc.vector, st, u, wt[0], DVE_PIECES, w_lo_done)

                    for b in range(GB):
                        statistics(0, b)
                        dve.wait_ge(s["stats_done"], b + 1)
                        moments(0, b)
                        centre(0, b)
                        norm(0, b)
                    dve.wait_ge(s_const, CONSTANTS)
                    run(dve, slot)

                @block.gpsimd
                def _(pool):
                    def root(g, b):
                        pool.wait_ge(s["aggr_done"], at(g * GB + b + 1))
                        nc.gpsimd.tensor_tensor(rstd[:, b], mv[:, b, 1:2], eps_t[:], ALU.add).then_inc(s["eps_added"], 1)
                        pool.wait_ge(s["eps_added"], at(g * GB + b + 1))
                        nc.gpsimd.tensor_tensor(rstd[:, b], rstd[:, b], neg_half[:], ALU.pow
                                                ).then_inc(s["rstd_done"], 1)

                    def prepare_mask(g, b):
                        k = 2 * (g * GB + b)
                        pool.wait_ge(mask_in[b], at(16 * (g + 1)))
                        if known(g, 1):
                            pool.wait_ge(s["biased"], at(slot_no(g - 1, NS - GB + b)))
                        nc.gpsimd.tensor_tensor(m_mul[:, b], m_raw[:, b], scale_t[:].to_broadcast([P, P]),
                                                ALU.mult).then_inc(s["mask_ready"], 1)
                        nc.gpsimd.tensor_scalar(m_add[:, b], m_raw[:, b], MASKED, -MASKED, ALU.mult,
                                                ALU.add).then_inc(s["mask_ready"], 1)

                    def add_bias(g, n):
                        b = n % GB
                        pool.wait_ge(s["masked"], at(slot_no(g, n)))
                        if n < GB:
                            pool.wait_ge(s["mask_ready"], at(2 * (g * GB + b + 1)))
                        nc.gpsimd.tensor_tensor(t_s[:, n % 2], t_s[:, n % 2],
                                                m_add[:, b].unsqueeze(1).to_broadcast([P, HQ, P]),
                                                ALU.add).then_inc(s["biased"], 1)

                    def value_last(g, b):
                        pool.wait_ge(s["v2_done"], at(g * GB + b + 1))
                        nc.gpsimd.tensor_tensor(v_b[:, b, :, 2 * HD:3 * HD],
                                                v_rest[:, b].rearrange("p (h d) -> p h d", h=NH),
                                                v_b[:, b, :, HD:2 * HD], ALU.subtract).then_inc(s["v3_done"], 1)

                    def value_rest(g, b):
                        pool.wait_ge(s["v1_done"], at(g * GB + b + 1))
                        v = v_rest[:, b].rearrange("p (h d) -> p h d", h=NH)
                        nc.gpsimd.tensor_tensor(v, v, v_b[:, b, :, 0:HD], ALU.subtract).then_inc(s["vr_done"], 1)

                    def output_row(g, b):
                        k = g * GB + b + 1
                        pool.wait_ge(s["y_copied"], at(k))
                        pool.wait_ge(s["res_ready"], at(k))
                        nc.gpsimd.tensor_tensor(y_t[:, b], y_t[:, b], res_t[:, b],
                                                ALU.add).then_inc(s["y_done"], 1)

                    def residual(g, b):
                        pool.wait_ge(res_in[b], at(16 * (g + 1)))
                        if b == 0 and opens(g):
                            pool.wait_ge(row_ready, 1 + crosses(g))
                        nc.gpsimd.tensor_tensor(res_t[:, b], res_t[:, b], bias_row[:, crosses(g)],
                                                ALU.add).then_inc(s["res_ready"], 1)

                    def slot(g, n, cur, prev, nxt):
                        if n in (2, 3) and cur and nxt:
                            root(g + 1, n - 2)
                        if n == 0 and cur:
                            prepare_mask(g, 1)
                        if n == 7 and nxt:
                            prepare_mask(g + 1, 0)
                        if n in (1, 3) and cur:
                            value_rest(g, n // 2)
                        if cur:
                            add_bias(g, n)
                        for st, u in units_split(g, n):
                            low_weights(nc.gpsimd, st, u, wt[0], POOL_PIECES, w_lo_pool)
                        if n in (1, 3) and cur:
                            value_last(g, n // 2)
                        if n in (5, 7) and prev:
                            output_row(g - 1, (n - 5) // 2)
                        if n in (4, 6) and prev:
                            residual(g - 1, (n - 4) // 2)

                    nc.gpsimd.memset(eps_t[:], EPS).then_inc(s_const, 1)
                    nc.gpsimd.memset(neg_half[:], -0.5).then_inc(s_const, 1)
                    nc.gpsimd.memset(ident[:], 0.0).then_inc(s_const, 1)
                    nc.gpsimd.memset(ones[:], 1.0).then_inc(s_const, 1)
                    nc.gpsimd.memset(scale_t[:], SCALE).then_inc(s_const, 1)
                    nc.gpsimd.memset(lift_t[:], LIFT).then_inc(s_const, 1)
                    pool.wait_ge(s_const, CONSTANTS - 1)
                    nc.gpsimd.affine_select(out=ident[:], in_=ident[:], compare_op=ALU.not_equal, fill=1.0,
                                            base=0, pattern=[[-1, P]], channel_multiplier=1).then_inc(s_const, 1)
                    root(0, 0)
                    root(0, 1)
                    nc.gpsimd.memset(k_bd[:].rearrange("p i h b t -> p (i h b t)").bitcast(F32),
                                     0.0).then_inc(s["kbd_clear"], 1)
                    for b in range(GB):
                        last = nc.gpsimd.memset(v_b[:, b, :, 3 * HD:VPAD], 1.0)
                    last.then_inc(s["ones_ready"], 1)
                    run(pool, slot)

        m_x_in = [sem(f"m_x_in{b}") for b in range(MB)]
        m_res_in = [sem(f"m_res_in{b}") for b in range(MB)]
        m_stored = [sem(f"m_stored{b}") for b in range(MB)]
        m_names = ("h_done gelu_done gh_done gl_done down_done m_xT_done m_xTh_done m_xTl_done m_stats_done "
                   "m_aggr_done m_centred m_eps_added m_rstd_done m_xn_done m_y_done m_res_ready")
        m = {name: sem(name) for name in m_names.split()}

        def mlp(st, x_src, dst):
            LAG = 2
            down_hi = sb("m_down_hi", [P, U, KC, H], F32R, st)
            w1 = (wt[0], wt[LOW_AT[UP]])
            w2 = (down_hi, wt[LOW_AT[DOWN]])
            TF = MB * P
            x_t = sb("m_x_t", [P, 2, H], F32, st)
            xn = sb("m_xn", [P, MB, H], F32, st)
            xT = sb("m_xT", [P, 2, KC, TF], F32R, st)
            res_t = sb("m_res_t", [P, MB, H], F32, st)
            g_t = sb("m_g_t", [P, 2, TF], F32, st)
            g_r = sb("m_g_r", [P, 2, 2, TF], F32R, st)
            stat = sb("m_stat", [P, MB, 6], F32, st)
            mv = sb("m_mv", [P, MB, 2], F32, st)
            rstd = sb("m_rstd", [P, MB, 1], F32, st)
            ps_h = [ps(f"m_ps_h{i}", [P, TF], F32, st) for i in range(2)]
            ps_x = [ps(f"m_ps_x{i}", [P, KC, P], F32, st) for i in range(2)]
            ps_y = [ps(f"m_ps_y{i}", [P, H], F32, st) for i in range(MB)]

            def known(g, least):
                return not isinstance(g, int) or g >= least

            def run(engine, steps):
                steps(-1, False, False, True)
                steps(0, True, False, True)
                if NM > 2:
                    with engine.Fori(0, NM - 2) as i:
                        steps(Looped(i, 1, 1), True, True, True)
                steps(NM - 1, True, True, False)

            def row(g, b):
                r = g * MB + b
                return r if isinstance(r, int) else bass.ds(at(r), 1)

            with nc.Block() as block:
                @block.sync
                def _(sp):
                    def load_x(g, b):
                        if b >= 2 or known(g, 1):
                            sp.wait_ge(m["m_xn_done"], at(g * MB + b - 1))
                        sp.dma_start(x_t[:, b % 2], x_src[row(g, b)]).then_inc(m_x_in[b], 16)

                    def load_res(g, b):
                        if known(g, 1):
                            sp.wait_ge(m_stored[b], at(16 * g))
                        sp.dma_start(res_t[:, b], x_src[row(g, b)]).then_inc(m_res_in[b], 16)

                    def store(g, b):
                        sp.wait_ge(m["m_y_done"], at(g * MB + b + 1))
                        sp.dma_start(dst[row(g, b)], res_t[:, b]).then_inc(m_stored[b], 16)

                    def steps(g, cur, prev, nxt):
                        if not cur:
                            for b in range(MB):
                                load_x(g + 1, b)
                            for c in range(KC):
                                load_raw(sp, DOWN, U - 1, c)
                            return
                        if prev:
                            for b in range(MB):
                                store(g - 1, b)
                        for b in range(MB):
                            load_res(g, b)
                        if nxt:
                            for b in range(MB):
                                load_x(g + 1, b)

                    run(sp, steps)
                    for b in range(MB):
                        store(NM - 1, b)
                    for b in range(MB):
                        sp.wait_ge(m_stored[b], at(16 * NM))

                @block.tensor
                def _(pe):
                    def up(g, j):
                        if j == 0:
                            pe.wait_ge(m["m_xTl_done"], at((g + 1) * MB))
                        if j >= 2 or known(g, 1):
                            pe.wait_ge(m["gelu_done"], at(g * FC + j - 1))
                        k = 0
                        for hw, hx in PASSES:
                            for kc in range(KC):
                                last = nc.tensor.matmul(
                                    ps_h[j % 2][:], w1[hw][:, j // KC, kc, (j % KC) * P:(j % KC + 1) * P],
                                    xT[:, hx, kc], start=(k == 0), stop=(k == 3 * KC - 1))
                                k += 1
                        last.then_inc(m["h_done"], 1)

                    def down(g, j, b):
                        if b == 0:
                            pe.wait_ge(m["gl_done"], at(g * FC + j + 1))
                            if j % KC == 0 and not known(g, 1):
                                wait_split(pe, DOWN, j // KC)
                        if j == 0 and known(g, 1):
                            pe.wait_ge(m["m_y_done"], at((g - 1) * MB + b + 1))
                        for x, (hg, hw) in enumerate(PASSES):
                            last = nc.tensor.matmul(ps_y[b][:], g_r[:, j % 2, hg, b * P:(b + 1) * P],
                                                    w2[hw][:, j // KC, j % KC],
                                                    start=(j == 0 and x == 0), stop=(j == FC - 1 and x == 2))
                        if b == MB - 1 or j == FC - 1:
                            last.then_inc(m["down_done"], 1)

                    def flip(g, b):
                        pe.wait_ge(m["m_xn_done"], at(g * MB + b + 1))
                        if b >= 2 or known(g, 1):
                            pe.wait_ge(m["m_xTl_done"], at(g * MB + b - 1))
                        for kc in range(KC):
                            last = nc.tensor.transpose(ps_x[b % 2][:, kc], xn[:, b, kc * P:(kc + 1) * P], ident[:])
                        last.then_inc(m["m_xT_done"], 1)

                    def steps(g, cur, prev, nxt):
                        if not cur:
                            for b in range(MB):
                                flip(g + 1, b)
                            return
                        for j in range(FC):
                            up(g, j)
                            if j >= LAG:
                                for b in range(MB):
                                    down(g, j - LAG, b)
                            if j >= FC - 2 and nxt:
                                flip(g + 1, j - FC + 2)
                        for b in range(MB):
                            down(g, FC - 2, b)
                            if b == 1 and nxt:
                                flip(g + 1, 2)
                        for b in range(MB):
                            if b == 1 and nxt:
                                flip(g + 1, 3)
                            down(g, FC - 1, b)

                    run(pe, steps)

                @block.scalar
                def _(act):
                    def gelu(g, j):
                        act.wait_ge(m["h_done"], at(g * FC + j + 1))
                        if j >= 2 or known(g, 1):
                            act.wait_ge(m["gl_done"], at(g * FC + j - 1))
                        nc.scalar.activation(g_t[:, j % 2], ps_h[j % 2][:], ACT.Gelu_apprx_tanh,
                                             bias=bias_cols[:, UP, j:j + 1]).then_inc(m["gelu_done"], 1)

                    def flip(g, b):
                        act.wait_ge(m["m_xT_done"], at(g * MB + b + 1))
                        if known(g, 1):
                            act.wait_ge(m["h_done"], at(g * FC))
                        nc.scalar.copy(xT[:, HI, :, b * P:(b + 1) * P], ps_x[b % 2][:]).then_inc(m["m_xTh_done"], 1)

                    def high(g, j):
                        act.wait_ge(m["gelu_done"], at(g * FC + j + 1))
                        if j >= 2:
                            act.wait_ge(m["down_done"], at(g * (FC + MB - 1) + j - 1))
                        elif known(g, 1):
                            act.wait_ge(m["down_done"], at(g * (FC + MB - 1) - (MB if j == 0 else 0)))
                        nc.scalar.copy(g_r[:, j % 2, HI], g_t[:, j % 2]).then_inc(m["gh_done"], 1)

                    def steps(g, cur, prev, nxt):
                        if cur:
                            for j in range(FC):
                                gelu(g, j)
                                high(g, j)
                                if j % KC == 0 and not known(g, 1):
                                    high_weights(act, DOWN, j // KC, down_hi)
                        if nxt:
                            for b in range(MB):
                                flip(g + 1, b)

                    run(act, steps)

                @block.vector
                def _(dve):
                    def low(g, j, stats=None):
                        if stats is not None:
                            dve.wait_ge(m["m_stats_done"], at(stats))
                        dve.wait_ge(m["gh_done"], at(g * FC + j + 1))
                        nc.vector.tensor_tensor(g_r[:, j % 2, LO], g_t[:, j % 2], g_r[:, j % 2, HI],
                                                ALU.subtract).then_inc(m["gl_done"], 1)

                    def flip(g, b):
                        dve.wait_ge(m["m_xTh_done"], at(g * MB + b + 1))
                        cols = slice(b * P, (b + 1) * P)
                        nc.vector.tensor_tensor(xT[:, LO, :, cols], ps_x[b % 2][:], xT[:, HI, :, cols],
                                                ALU.subtract).then_inc(m["m_xTl_done"], 1)

                    def statistics(g, b):
                        dve.wait_ge(m_x_in[b], at(16 * (g + 1)))
                        nc.vector.bn_stats(stat[:, b], x_t[:, b % 2]).then_inc(m["m_stats_done"], 1)

                    def norm(g, b):
                        k = g * MB + b + 1
                        nc.vector.bn_aggr(mv[:, b], stat[:, b]).then_inc(m["m_aggr_done"], 1)
                        dve.wait_ge(m["m_aggr_done"], at(k))
                        if known(g, 1):
                            dve.wait_ge(m["m_xT_done"], at(k - MB))
                        nc.vector.scalar_tensor_tensor(
                            out=xn[:, b], in0=x_t[:, b % 2], scalar=mv[:, b, 0:1], in1=norm_row[:, 0],
                            op0=ALU.subtract, op1=ALU.mult).then_inc(m["m_centred"], 1)
                        dve.wait_ge(m["m_centred"], at(k))
                        dve.wait_ge(m["m_rstd_done"], at(k))
                        nc.vector.scalar_tensor_tensor(
                            out=xn[:, b], in0=xn[:, b], scalar=rstd[:, b], in1=norm_row[:, 1],
                            op0=ALU.mult, op1=ALU.add).then_inc(m["m_xn_done"], 1)

                    def output_row(g, b):
                        dve.wait_ge(m["down_done"], at(g * (FC + MB - 1) + FC + b))
                        dve.wait_ge(m["m_res_ready"], at(g * MB + b + 1))
                        nc.vector.tensor_tensor(res_t[:, b], ps_y[b][:], res_t[:, b],
                                                ALU.add).then_inc(m["m_y_done"], 1)

                    def steps(g, cur, prev, nxt):
                        if not cur:
                            dve.wait_ge(norm_in, 96)
                            for b in range(MB):
                                statistics(g + 1, b)
                                dve.wait_ge(m["m_stats_done"], (g + 1) * MB + b + 1)
                                norm(g + 1, b)
                        if cur:
                            for j in range(FC):
                                b = j - 4
                                norms_next = nxt and 0 <= b < MB
                                if norms_next:
                                    statistics(g + 1, b)
                                low(g, j, (g + 1) * MB + b + 1 if norms_next else None)
                                if norms_next:
                                    norm(g + 1, b)
                                if j % KC == 0 and not known(g, 1):
                                    low_weights(nc.vector, DOWN, j // KC, down_hi, DVE_PIECES, w_lo_done)
                        if nxt:
                            for b in range(MB):
                                flip(g + 1, b)
                        if cur:
                            for b in range(MB):
                                output_row(g, b)

                    run(dve, steps)

                @block.gpsimd
                def _(pool):
                    def root(g, b):
                        pool.wait_ge(m["m_aggr_done"], at(g * MB + b + 1))
                        nc.gpsimd.tensor_tensor(rstd[:, b], mv[:, b, 1:2], eps_t[:], ALU.add
                                                ).then_inc(m["m_eps_added"], 1)
                        pool.wait_ge(m["m_eps_added"], at(g * MB + b + 1))
                        nc.gpsimd.tensor_tensor(rstd[:, b], rstd[:, b], neg_half[:], ALU.pow
                                                ).then_inc(m["m_rstd_done"], 1)

                    def steps(g, cur, prev, nxt):
                        if cur:
                            for b in range(MB):
                                pool.wait_ge(m_res_in[b], at(16 * (g + 1)))
                                nc.gpsimd.tensor_tensor(res_t[:, b], res_t[:, b], bias_row[:, UP],
                                                        ALU.add).then_inc(m["m_res_ready"], 1)
                        if cur and not known(g, 1):
                            low_weights(nc.gpsimd, DOWN, 0, down_hi, POOL_PIECES, w_lo_pool)
                            root(g + 1, 0)
                            low_weights(nc.gpsimd, DOWN, 1, down_hi, POOL_PIECES, w_lo_pool)
                            for b in range(1, MB):
                                root(g + 1, b)
                            for u in range(2, U):
                                low_weights(nc.gpsimd, DOWN, u, down_hi, POOL_PIECES, w_lo_pool)
                        elif nxt:
                            for b in range(MB):
                                root(g + 1, b)

                    run(pool, steps)

        with ExitStack() as st:
            attention(st)
        with ExitStack() as st:
            mlp(st, x2_dram, out)


_NAMES = {
    "x": "x", "ctx": "ctx_2048", "mask_self": "mask_1x1xSxS2_fc1", "mask_cross": "mask_Bx1xSxS2_ff1",
    **{n: f"L0_xattn_{n}" for n in ("ln1_s", "ln1_b", "w_qkv", "b_qkv", "w_ao", "b_ao", "ln2_s", "ln2_b", "w_q",
                                    "b_q", "w_kv", "b_kv", "w_co", "b_co", "ln3_s", "ln3_b", "w1", "b1", "w2",
                                    "b2")},
}


def kernel(**inputs):
    import numpy as _np
    import concourse.bacc as _bacc
    from concourse.bass_utils import run_bass_kernel_spmd as _run

    nc = _bacc.Bacc("TRN2", target_bir_lowering=False, num_devices=1)
    arrays, args = {}, {}
    for short, name in _NAMES.items():
        v = _np.ascontiguousarray(inputs[name])
        arrays[f"in_{short}"] = v
        args[short] = nc.dram_tensor(f"in_{short}", v.shape, mybir.dt.from_np(v.dtype), kind="ExternalInput").ap()
    shape = arrays["in_x"].shape
    out = nc.dram_tensor("out", shape, F32, kind="ExternalOutput").ap()
    xattn_layer(nc, args, out)
    r = _run(nc, [arrays], core_ids=[0])
    return r.results[0]["out"]
```
